# Optimizing a Trainium2 kernel written in Bass

```python
import numpy as np
import jax
import jax.numpy as jnp

def _softmax(x, axis=-1):
    return jax.nn.softmax(x, axis=axis)

def _gelu(x):
    return jax.nn.gelu(x, approximate=True)

def _silu(x):
    return jax.nn.silu(x)

def _sigmoid(x):
    return jax.nn.sigmoid(x)

def _layernorm(x, axis=-1, eps=1e-05):
    m = jnp.mean(x, axis=axis, keepdims=True)
    v = jnp.var(x, axis=axis, keepdims=True)
    return (x - m) / jnp.sqrt(v + eps)

def _scatter_add(tgt, idx, src, axis=0):
    return tgt.at[idx].add(src)

def _segment_sum(src, seg, n):
    return jax.ops.segment_sum(src, seg, n)
kernel_name = 'mk_gnn_resnorm_d2_gnn_r32_285f93'

def setup_inputs(seed: int=0):
    np.random.seed(seed)
    _w = jnp.asarray

    def _rec_inputs():
        import jax
        import jax.numpy as jnp
        _gk = jax.random.key(seed)
        x = -0.0005121 + 1.001 * jax.random.normal(jax.random.fold_in(_gk, 1), (50000, 64), jnp.float32)
        src = jax.random.randint(jax.random.fold_in(_gk, 2), (50000,), 0, 50000, jnp.int32)
        dst = jax.random.randint(jax.random.fold_in(_gk, 3), (50000,), 0, 50000, jnp.int32)
        _o = jnp.argsort(dst, stable=True)
        src = src[_o]
        dst = dst[_o]
        edge_attr_64 = -9.77346e-05 + 0.999888 * jax.random.normal(jax.random.fold_in(_gk, 12), (50000, 64), jnp.float32)
        return (x, src, dst, edge_attr_64)
    x, src, dst, edge_attr_64 = _rec_inputs()

    def _L0_gnn_setup():
        import jax, jax.numpy as jnp
        import numpy as np
        N = 50000
        E = 25000
        D = 64
        L = 3
        LN_EPS = 1e-05

        def _transformer_conv(x, src, dst, edge_attr, Wq, bq, Wk, bk, Wv, bv, We, Ws, bs):
            q = x @ Wq + bq
            k = x @ Wk + bk
            v = x @ Wv + bv
            e = edge_attr @ We
            kj = k[src] + e
            alpha = jnp.sum(q[dst] * kj, axis=-1) / jnp.sqrt(jnp.float32(D))
            amax = jax.ops.segment_max(alpha, dst, num_segments=N)
            p = jnp.exp(alpha - amax[dst])
            denom = jax.ops.segment_sum(p, dst, num_segments=N)
            w = p / denom[dst]
            msg = (v[src] + e) * w[:, None]
            agg = jax.ops.segment_sum(msg, dst, num_segments=N)
            return agg + x @ Ws + bs

        def _layer_norm(x, gamma, beta):
            mu = jnp.mean(x, axis=-1, keepdims=True)
            var = jnp.mean(jnp.square(x - mu), axis=-1, keepdims=True)
            return (x - mu) * jax.lax.rsqrt(var + LN_EPS) * gamma + beta
        key = jax.random.key(seed)
        ks = jax.random.split(key, 16)
        s = 1.0 / np.sqrt(D)
        node_attr = jax.random.normal(ks[0], (N, D), dtype=jnp.float32)
        edge_attr = jax.random.normal(ks[1], (E, D), dtype=jnp.float32)
        edge_index = jax.random.randint(ks[2], (2, E), 0, N, dtype=jnp.int32)
        mk = lambda k: jax.random.normal(k, (L, D, D), dtype=jnp.float32) * s
        return {'node_attr': node_attr, 'edge_index': edge_index, 'edge_attr': edge_attr, 'Wq': mk(ks[3]), 'bq': jnp.zeros((L, D), jnp.float32), 'Wk': mk(ks[4]), 'bk': jnp.zeros((L, D), jnp.float32), 'Wv': mk(ks[5]), 'bv': jnp.zeros((L, D), jnp.float32), 'We': mk(ks[6]), 'Ws': mk(ks[7]), 'bs': jnp.zeros((L, D), jnp.float32), 'ln_gamma': jnp.ones((L - 1, D), jnp.float32), 'ln_beta': jnp.zeros((L - 1, D), jnp.float32)}
    _L0_gnn_all = _L0_gnn_setup()
    _L0_gnn_in = {k: v for k, v in _L0_gnn_all.items() if k in ('Wq', 'bq', 'Wk', 'bk', 'Wv', 'bv', 'We', 'Ws', 'bs', 'ln_gamma', 'ln_beta')}
    del _L0_gnn_all

    def _L1_gnn_setup():
        import jax, jax.numpy as jnp
        import numpy as np
        N_NODES = 50000
        N_EDGES = 25000
        DIM = 64
        N_HEADS = 4

        def _scatter_softmax(scores, dst, n_nodes):
            m = jax.ops.segment_max(scores, dst, num_segments=n_nodes)
            m = jnp.maximum(m, jnp.float32(-1000000000.0))
            ex = jnp.exp(scores - m[dst])
            denom = jax.ops.segment_sum(ex, dst, num_segments=n_nodes)
            return ex / (denom[dst] + 1e-09)
        key = jax.random.key(seed)
        ks = jax.random.split(key, 7)
        x = jax.random.normal(ks[0], (N_NODES, DIM), dtype=jnp.float32)
        Wq = jax.random.normal(ks[1], (DIM, DIM), dtype=jnp.float32) / np.sqrt(DIM)
        Wk = jax.random.normal(ks[2], (DIM, DIM), dtype=jnp.float32) / np.sqrt(DIM)
        Wv = jax.random.normal(ks[3], (DIM, DIM), dtype=jnp.float32) / np.sqrt(DIM)
        Wo = jax.random.normal(ks[4], (DIM, DIM), dtype=jnp.float32) / np.sqrt(DIM)
        src = jax.random.randint(ks[5], (N_EDGES,), 0, N_NODES, dtype=jnp.int32)
        dst = jax.random.randint(ks[6], (N_EDGES,), 0, N_NODES, dtype=jnp.int32)
        return {'x': x, 'Wq': Wq, 'Wk': Wk, 'Wv': Wv, 'Wo': Wo, 'src': src, 'dst': dst}
    _L1_gnn_all = _L1_gnn_setup()
    _L1_gnn_in = {k: v for k, v in _L1_gnn_all.items() if k in ('Wq', 'Wk', 'Wv', 'Wo')}
    del _L1_gnn_all
    return {'x': x, 'src': src, 'dst': dst, 'edge_attr_64': edge_attr_64, 'L0_gnn_Wq': _L0_gnn_in['Wq'], 'L0_gnn_bq': _L0_gnn_in['bq'], 'L0_gnn_Wk': _L0_gnn_in['Wk'], 'L0_gnn_bk': _L0_gnn_in['bk'], 'L0_gnn_Wv': _L0_gnn_in['Wv'], 'L0_gnn_bv': _L0_gnn_in['bv'], 'L0_gnn_We': _L0_gnn_in['We'], 'L0_gnn_Ws': _L0_gnn_in['Ws'], 'L0_gnn_bs': _L0_gnn_in['bs'], 'L0_gnn_ln_gamma': _L0_gnn_in['ln_gamma'], 'L0_gnn_ln_beta': _L0_gnn_in['ln_beta'], 'L1_gnn_Wq': _L1_gnn_in['Wq'], 'L1_gnn_Wk': _L1_gnn_in['Wk'], 'L1_gnn_Wv': _L1_gnn_in['Wv'], 'L1_gnn_Wo': _L1_gnn_in['Wo']}

def reference(x, src, dst, edge_attr_64, L0_gnn_Wq, L0_gnn_bq, L0_gnn_Wk, L0_gnn_bk, L0_gnn_Wv, L0_gnn_bv, L0_gnn_We, L0_gnn_Ws, L0_gnn_bs, L0_gnn_ln_gamma, L0_gnn_ln_beta, L1_gnn_Wq, L1_gnn_Wk, L1_gnn_Wv, L1_gnn_Wo):
    import jax
    import jax.numpy as jnp

    def _L0_gnn_ref(node_attr, edge_index, edge_attr, Wq, bq, Wk, bk, Wv, bv, We, Ws, bs, ln_gamma, ln_beta):
        import jax, jax.numpy as jnp
        import numpy as np
        N = 50000
        E = 25000
        D = 64
        L = 3
        LN_EPS = 1e-05

        def _transformer_conv(x, src, dst, edge_attr, Wq, bq, Wk, bk, Wv, bv, We, Ws, bs):
            q = x @ Wq + bq
            k = x @ Wk + bk
            v = x @ Wv + bv
            e = edge_attr @ We
            kj = k[src] + e
            alpha = jnp.sum(q[dst] * kj, axis=-1) / jnp.sqrt(jnp.float32(D))
            amax = jax.ops.segment_max(alpha, dst, num_segments=N)
            p = jnp.exp(alpha - amax[dst])
            denom = jax.ops.segment_sum(p, dst, num_segments=N)
            w = p / denom[dst]
            msg = (v[src] + e) * w[:, None]
            agg = jax.ops.segment_sum(msg, dst, num_segments=N)
            return agg + x @ Ws + bs

        def _layer_norm(x, gamma, beta):
            mu = jnp.mean(x, axis=-1, keepdims=True)
            var = jnp.mean(jnp.square(x - mu), axis=-1, keepdims=True)
            return (x - mu) * jax.lax.rsqrt(var + LN_EPS) * gamma + beta
        src, dst = (edge_index[0], edge_index[1])
        x = node_attr
        for i in range(L):
            x = _transformer_conv(x, src, dst, edge_attr, Wq[i], bq[i], Wk[i], bk[i], Wv[i], bv[i], We[i], Ws[i], bs[i])
            x = jax.nn.relu(x)
            if i < L - 1:
                x = _layer_norm(x, ln_gamma[i], ln_beta[i])
        return jax.nn.log_softmax(x, axis=1)

    def _L1_gnn_ref(x, Wq, Wk, Wv, Wo, src, dst):
        import jax, jax.numpy as jnp
        import numpy as np
        N_NODES = 50000
        N_EDGES = 25000
        DIM = 64
        N_HEADS = 4

        def _scatter_softmax(scores, dst, n_nodes):
            m = jax.ops.segment_max(scores, dst, num_segments=n_nodes)
            m = jnp.maximum(m, jnp.float32(-1000000000.0))
            ex = jnp.exp(scores - m[dst])
            denom = jax.ops.segment_sum(ex, dst, num_segments=n_nodes)
            return ex / (denom[dst] + 1e-09)
        N, D = x.shape
        H = N_HEADS
        Dh = D // H
        q = (x @ Wq).reshape(N, H, Dh)
        k = (x @ Wk).reshape(N, H, Dh)
        v = (x @ Wv).reshape(N, H, Dh)
        scores = jnp.einsum('ehd,ehd->eh', q[dst], k[src]) / jnp.sqrt(jnp.float32(Dh))
        alpha = _scatter_softmax(scores, dst, N)
        agg = jax.ops.segment_sum(alpha[:, :, None] * v[src], dst, num_segments=N)
        return agg.reshape(N, D) @ Wo
    edge_index = jnp.stack([src, dst])
    x = _layernorm(x + _L0_gnn_ref(x, edge_index, edge_attr_64, L0_gnn_Wq, L0_gnn_bq, L0_gnn_Wk, L0_gnn_bk, L0_gnn_Wv, L0_gnn_bv, L0_gnn_We, L0_gnn_Ws, L0_gnn_bs, L0_gnn_ln_gamma, L0_gnn_ln_beta), axis=-1)
    x = _layernorm(x + _L1_gnn_ref(x, L1_gnn_Wq, L1_gnn_Wk, L1_gnn_Wv, L1_gnn_Wo, src, dst), axis=-1)
    return x

_drawn_inputs = setup_inputs


def setup_inputs(seed=0):
    import zlib

    import numpy as np

    out = dict(_drawn_inputs(seed))
    spreads = {'L0_gnn_bq': (0.0, 0.1),
     'L0_gnn_bk': (0.0, 0.1),
     'L0_gnn_bv': (0.0, 0.1),
     'L0_gnn_bs': (0.0, 0.1),
     'L0_gnn_ln_gamma': (1.0, 0.2),
     'L0_gnn_ln_beta': (0.0, 0.1)}
    factors = {}
    for name, (base, spread) in spreads.items():
        noise = np.random.default_rng([zlib.crc32(name.encode()), seed]).standard_normal(out[name].shape)
        drawn = base * np.exp(spread * noise) if base else spread * noise
        out[name] = jnp.asarray(drawn.astype(out[name].dtype))
    for name, factor in factors.items():
        out[name] = (out[name] * factor).astype(out[name].dtype)
    return out
```

```python
from contextlib import ExitStack

import concourse.bass as bass
from concourse import mybir

F32 = mybir.dt.float32
BF16 = mybir.dt.bfloat16
I32 = mybir.dt.int32
ALU = mybir.AluOpType
ACT = mybir.ActivationFunctionType
AX = mybir.AxisListType

P = 128
D = 64
C = 4
MAPC = 14
NODEC = 8
SPLIT = 112
NEVER = -1.0e30
SKIP = 1 << 20
HEADW = 16
LAYERS = (0, 1, 2, 3)


class Half:

    def __init__(self, i, par):
        self.i, self.par = i, par
        self.k = 2 * i + par

    def plus(self, off):
        n = self.par + off
        return Half(self.i + n // 2, n % 2)

    def exists(self, halves):
        return not isinstance(self.k, int) or 0 <= self.k < halves

    def cols(self):
        return bass.ds(self.k * C, C)


class Signal:

    def __init__(self, sem, halves, step=1, layers=LAYERS):
        self.sem, self.halves, self.step, self.layers = sem, halves, step, layers

    def at(self, layer, k, n=None):
        before = self.halves * sum(x < layer for x in self.layers)
        return k * self.step + (before * self.step + (self.step if n is None else n))


class Landing:

    def __init__(self, sems, halves, step=16, layers=LAYERS):
        self.sem, self.halves, self.step, self.layers = sems, halves, step, layers

    def at(self, layer, i):
        before = self.halves // 2 * sum(x < layer for x in self.layers)
        return i * self.step + (before + 1) * self.step


def wait(eng, sem, value):
    if not isinstance(value, int) or value > 0:
        eng.wait_ge(sem, value)


def after(eng, signal, layer, h):
    wait(eng, signal.sem, signal.at(layer, h.k))


def landed(eng, landing, layer, h):
    wait(eng, landing.sem[h.par], landing.at(layer, h.i))


def run(eng, halves, step, lo, hi):
    start, stop = 3, (halves - 3) // 2
    for s in range(lo, 2 * start):
        step(Half(s // 2, s % 2))
    with eng.Fori(start, stop) as i:
        step(Half(i, 0))
        step(Half(i, 1))
    for s in range(2 * stop, hi + 1):
        step(Half(s // 2, s % 2))


def stage(fn, h, off, halves):
    h = h.plus(off)
    if h.exists(halves):
        fn(h)


def gnn_kernel(nc, x, src, dst, edge_attr, Wq, bq, Wk, bk, Wv, bv, We, Ws, bs, gamma, beta, Wq1, Wk1, Wv1, Wo1, out):
    N, E = x.shape[0], src.shape[0]
    COLS = -(-E // (P * 2 * C)) * 2 * C
    HALVES = COLS // C
    EP = P * COLS
    LASTC = E - (P - 1) * COLS
    FULL = LASTC // C
    MAPH = COLS // MAPC
    BLOCK = P * NODEC
    BLOCKS = -(-N // BLOCK)
    TAILP = (N - (BLOCKS - 1) * BLOCK) // NODEC
    RUN = -(-N // P)
    while N % RUN:
        RUN += 1
    NH = D // HEADW
    R = D + NH
    assert LASTC % C == 0 and LASTC > 0 and COLS % MAPC == 0 and MAPH % 2 == 0 and HALVES % 2 == 0
    assert (BLOCKS - 1) * BLOCK + TAILP * NODEC == N and E % 16 == 0

    rows = [x] + [nc.dram_tensor(f"rows{l}", (N + EP, D), F32, kind="Internal").ap() for l in (1, 2, 3)]
    acc_d = nc.dram_tensor("acc_rows", (EP, D), F32, kind="Internal").ap()
    skip_d = nc.dram_tensor("skip_rows", (EP, D), F32, kind="Internal").ap()
    x0_d = nc.dram_tensor("x_at_dst", (EP, D), F32, kind="Internal").ap()
    etail_d = nc.dram_tensor("edge_tail", ((P - SPLIT) * COLS, D), F32, kind="Internal").ap()
    dpad = nc.dram_tensor("dst_padded", (EP + 2,), I32, kind="Internal").ap()
    where_d = nc.dram_tensor("row_of_node", (N, 1), I32, kind="Internal").ap()

    def by_edge(t):
        return t.rearrange("(p j) d -> p j d", p=P)

    with ExitStack() as ctx:
        def sb(name, shape, dt=F32):
            return ctx.enter_context(nc.sbuf_tensor(name, shape, dt))

        def sem(name):
            return ctx.enter_context(nc.semaphore(name))

        def signal(name, layers=LAYERS, step=1):
            return Signal(sem(name), HALVES, step, layers)

        def landing(name, layers=LAYERS, step=16):
            return Landing([sem(name + "_a"), sem(name + "_b")], HALVES, step, layers)

        def event(name, layers=LAYERS, step=1):
            return Signal(sem(name), 1, step, layers)

        feats = sb("feats", [P, COLS, D])
        src_i = sb("src_i", [P, COLS], I32)
        row_i = sb("row_i", [P, COLS], I32)
        cont = sb("cont", [P, COLS])
        notlast = sb("notlast", [P, COLS])
        pen = sb("pen", [P, COLS])
        lead = sb("lead", [P, COLS])
        leadend = sb("leadend", [P, COLS])
        ownlast = sb("ownlast", [P, COLS])
        out_i = sb("out_i", [P, COLS], I32)
        M = sb("M", [P, NH, COLS + 1])
        S = sb("S", [P, NH, COLS + 1])
        ident = sb("ident", [P, P])
        eps = sb("eps", [P, 1])
        ones3 = sb("ones3", [3, P], BF16)
        wkv = sb("wkv", [P, 3, 2 * D])
        wqs = sb("wqs", [P, 3, 2, 2 * D])
        wkv1 = sb("wkv1", [P, 2, 2 * D])
        wq1 = sb("wq1", [P, 2, D])
        wo1 = sb("wo1", [P, 2, D])
        gam = sb("gam", [P, 2])
        bet = sb("bet", [P, 2])
        bias3 = sb("bias3", [3, 3, 2, C, 2 * D], BF16)
        lead_i = sb("lead_i", [P, 3], I32)
        ends = sb("ends", [P, 4])
        fix = sb("fix", [P, D])
        dst_i = sb("dst_i", [P, COLS], I32)
        end_i = sb("end_i", [P, COLS], I32)
        pos_i = sb("pos_i", [P, COLS], I32)
        ctile = {s: sb("c_" + s, [R, P]) for s in ("m", "a", "mF", "f", "wpen", "cpen", "noend", "d1", "d2", "e1", "e2", "t")}
        idxr = sb("idxr", [P, 2, 2, C], I32)
        T = sb("T", [P, 2, C, 2, D])
        T3 = T[:].rearrange("p r c t d -> p r (c t) d")
        xs = sb("xs", [P, 2, C, D])
        fT = sb("fT", [P, 2, C * P])
        xT = sb("xT", [P, 2, 2 * P])
        qs = sb("qs", [P, 2, C, 2 * D])
        alpha = sb("alpha", [P, 2, NH * C])
        dif = sb("dif", [P, 2, 2, NH * C])
        ex = sb("ex", [P, 2, 2, NH * C])
        acc = sb("acc", [P, 2 * C, D])
        cen = sb("cen", [P, 2, C, D])
        var = sb("var", [P, 2, C])
        rstd = sb("rstd", [P, 2, C])
        x0 = sb("x0", [P, 2, C, D])
        yout = sb("yout", [P, 2, C, D])
        oidx = sb("oidx", [P, 2, C], I32)
        leadx = sb("leadx", [P, C, D])
        prod = sb("prod", [P, C, D])
        alphac = sb("alphac", [P, NH * C])
        dif0 = sb("dif0", [P, NH * C])
        pv = sb("pv", [P, C, D])
        carry = sb("carry", [P, D])
        stot = sb("stot", [P, NH * C])
        sinv = sb("sinv", [P, NH * C])
        t1 = sb("t1", [P, C, D])
        t2 = sb("t2", [P, C, D])
        t3 = sb("t3", [P, C, D])
        ez = sb("ez", [P, C, D])
        junk = sb("junk", [P, C, D])
        agT = sb("agT", [P, 2 * P])
        csum = sb("csum", [P, C])
        mean = sb("mean", [P, C])
        hmax = sb("hmax", [P, C])
        esum = sb("esum", [P, C])
        lns = sb("lns", [P, C])
        lnv = sb("lnv", [P, C])
        rmask = sb("rmask", [P, C])

        psT = [ctx.enter_context(nc.psum_tensor(f"psT{i}", [P, 512], F32)) for i in (0, 1)]
        psX = [ctx.enter_context(nc.psum_tensor(f"psX{i}", [P, 512], F32)) for i in (0, 1)]
        psKV = [ctx.enter_context(nc.psum_tensor(f"psKV{i}", [P, 512], F32)) for i in (0, 1)]
        psQ = [ctx.enter_context(nc.psum_tensor(f"psQ{i}", [P, 512], F32)) for i in (0, 1)]

        with ExitStack() as tmp:
            def ts(name, shape, dt=F32):
                return tmp.enter_context(nc.sbuf_tensor(name, shape, dt))

            cur = ts("cur", [P, COLS], I32)
            nxt = ts("nxt", [P, COLS], I32)
            prv = ts("prv", [P, COLS], I32)
            padi = ts("padi", [1, EP - E + 2], I32)
            nodes = ts("nodes", [P, RUN], I32)
            last = ts("last", [P, COLS])
            zeros = ts("zeros", [P, COLS])
            f1 = ts("f1", [P, COLS])
            f2 = ts("f2", [P, COLS])
            brow = ts("brow", [1, 3, 4 * D])
            bsplit = ts("bsplit", [1, 3, 3, 4 * D], BF16)
            bres = ts("bres", [1, 3, 4 * D])
            lead_f = ts("lead_f", [P, 3])
            flagrows = ts("flagrows", [P, 3, R])
            flags_made, flags_T = sem("flags_made"), sem("flags_T")
            loaded, zeroed, padded, shifted = sem("loaded"), sem("zeroed"), sem("padded"), sem("shifted")
            split_ready, bias_in, consts, table_in = sem("split_ready"), sem("bias_in"), sem("consts"), sem("table_in")
            bias_mm, setup_n = sem("bias_mm"), sem("setup_n")

            w3 = "l a b -> a l b"
            jobs = [(wkv[0:D, :, 0:D], Wk.rearrange(w3)), (wkv[0:D, :, D:2 * D], Wv.rearrange(w3)),
                    (wkv[D:P, :, 0:D], We.rearrange(w3)), (wkv[D:P, :, D:2 * D], We.rearrange(w3))]
            for b in (0, D):
                j = b // D
                jobs += [(wqs[b:b + D, :, j, 0:D], Wq.rearrange(w3)), (wqs[b:b + D, :, j, D:2 * D], Ws.rearrange(w3)),
                         (wkv1[b:b + D, j, 0:D], Wk1), (wkv1[b:b + D, j, D:2 * D], Wv1),
                         (wq1[b:b + D, j, :], Wq1), (wo1[b:b + D, j, :], Wo1)]
                for l in (0, 1):
                    jobs += [(gam[b:b + D, l:l + 1], gamma[l:l + 1, :].rearrange("l d -> d l")),
                             (bet[b:b + D, l:l + 1], beta[l:l + 1, :].rearrange("l d -> d l"))]
            for j, bias in enumerate((bk, bv, bq, bs)):
                jobs += [(brow[:, :, j * D:(j + 1) * D], bias.rearrange("(a l) d -> a l d", a=1))]
            jobs += [(src_i[0:SPLIT, :], src[0:SPLIT * COLS].rearrange("(p j) -> p j", j=COLS)),
                     (src_i[SPLIT:P - 1, :], src[SPLIT * COLS:(P - 1) * COLS].rearrange("(p j) -> p j", j=COLS)),
                     (src_i[P - 1:P, 0:LASTC], src[(P - 1) * COLS:E].rearrange("(p j) -> p j", p=1))]
            with nc.Block() as block:
                @block.sync
                def _(sp):
                    sp.wait_ge(zeroed, 1)
                    for tile, source in jobs:
                        sp.dma_start(tile, source).then_inc(loaded, 16)
                    sp.wait_ge(loaded, 16 * len(jobs))
                    sp.dma_start(etail_d[0:E - SPLIT * COLS, :].rearrange("(a n) d -> a (n d)", a=16),
                                 edge_attr[SPLIT * COLS:E, :].rearrange("(a n) d -> a (n d)", a=16)).then_inc(padded, 16)
                    sp.dma_start(etail_d[E - SPLIT * COLS:, :].rearrange("r d -> (r d)").rearrange("(p n) -> p n", p=P),
                                 zeros[:, 0:(EP - E) * D // P]).then_inc(padded, 16)
                    sp.dma_start(dpad[1:E + 1].rearrange("(a n) -> a n", a=16), dst.rearrange("(a n) -> a n", a=16)).then_inc(padded, 16)
                    sp.dma_start(dpad[0:1].rearrange("(a n) -> a n", a=1), padi[:, 0:1]).then_inc(padded, 16)
                    sp.dma_start(dpad[E + 1:EP + 1].rearrange("(a n) -> a n", a=1), padi[:, 1:EP - E + 1]).then_inc(padded, 16)
                    sp.dma_start(dpad[EP + 1:EP + 2].rearrange("(a n) -> a n", a=1), padi[:, 0:1]).then_inc(padded, 16)
                    sp.wait_ge(padded, 96)
                    for off, tile in ((1, cur), (2, nxt), (0, prv)):
                        sp.dma_start(tile[:, :], dpad[off:off + EP].rearrange("(p j) -> p j", p=P)).then_inc(shifted, 16)
                    sp.wait_ge(split_ready, 1)
                    for part in range(3):
                        for c in range(C):
                            for l in range(3):
                                sp.dma_start(bias3[part:part + 1, l, :, c, :],
                                             bsplit[0:1, part, l, :].rearrange("o (t d) -> o t d", t=2)).then_inc(bias_in, 16)
                    sp.wait_ge(bias_in, 16 * 9 * C)

                @block.gpsimd
                def _(pool):
                    nc.gpsimd.memset(ident[:, :], 0.0).then_inc(consts, 1)
                    pool.wait_ge(consts, 1)
                    nc.gpsimd.affine_select(out=ident[:, :], in_=ident[:, :], compare_op=ALU.not_equal, fill=1.0, base=0,
                                            pattern=[[-1, P]], channel_multiplier=1).then_inc(consts, 1)
                    nc.gpsimd.iota(pos_i[:, :], pattern=[[1, COLS]], base=N, channel_multiplier=COLS).then_inc(consts, 1)
                    nc.gpsimd.iota(nodes[:, :], pattern=[[1, RUN]], base=0, channel_multiplier=RUN).then_inc(consts, 1)
                    pool.wait_ge(consts, 4)
                    pool.dma_start(where_d.rearrange("(p j) o -> p (j o)", j=RUN), nodes[0:N // RUN, :]).then_inc(table_in, 16)
                    pool.wait_ge(table_in, 16)

                @block.tensor
                def _(pe):
                    pe.wait_ge(loaded, 16 * len(jobs))
                    for l in (1, 2):
                        nc.tensor.matmul(psQ[l - 1][0:1, 0:2 * D], bet[0:D, l - 1:l], wkv[0:D, l, :], start=True, stop=True)
                        nc.tensor.matmul(psQ[l - 1][0:1, 2 * D:4 * D], bet[0:D, l - 1:l], wqs[0:D, l, 0, :],
                                         start=True, stop=True).then_inc(bias_mm, 1)
                    pe.wait_ge(flags_made, 1)
                    pe.wait_ge(consts, 4)
                    for j in range(3):
                        ins = nc.tensor.transpose(psT[0][0:R, j * P:(j + 1) * P], flagrows[:, j, :], ident[:, :])
                    ins.then_inc(flags_T, 1)

                @block.vector
                def _(dve):
                    done = [0]

                    def link(ins):
                        done[0] += 1
                        ins.then_inc(setup_n, 1)
                        dve.wait_ge(setup_n, done[0])

                    for tile, value in ((src_i, 0), (eps, 1e-5), (ones3, 1.0), (T, 0.0), (xs, 0.0), (acc, 0.0),
                                        (fix, 0.0), (zeros, 0.0), (qs, 0.0),
                                        (wqs, 0.0), (wkv1, 0.0), (wq1, 0.0), (wo1, 0.0)):
                        nc.vector.memset(tile[:], value)
                    nc.vector.memset(feats[:, 0:2 * NODEC, :], 0.0)
                    nc.vector.memset(M[:, :, 0:1], NEVER)
                    nc.vector.memset(S[:, :, 0:1], 0.0)
                    nc.vector.memset(padi[:, 0:1], N + 1)
                    nc.vector.memset(padi[:, 1:], N).then_inc(zeroed, 1)
                    dve.wait_ge(zeroed, 1)
                    dve.wait_ge(loaded, 16 * len(jobs))
                    dve.wait_ge(bias_mm, 2)
                    for l in (1, 2):
                        link(nc.vector.tensor_tensor(brow[:, l, :], brow[:, l, :], psQ[l - 1][0:1, 0:4 * D], ALU.add))
                        link(nc.vector.tensor_scalar(wkv[0:D, l, :], wkv[0:D, l, :], gam[0:D, l - 1:l], None, ALU.mult))
                        link(nc.vector.tensor_scalar(wqs[:, l, :, :], wqs[:, l, :, :], gam[:, l - 1:l], None, ALU.mult))
                    link(nc.vector.tensor_copy(bsplit[:, 0], brow[:]))
                    link(nc.vector.tensor_tensor(bres[:], brow[:], bsplit[:, 0], ALU.subtract))
                    link(nc.vector.tensor_copy(bsplit[:, 1], bres[:]))
                    link(nc.vector.tensor_tensor(bres[:], bres[:], bsplit[:, 1], ALU.subtract))
                    nc.vector.tensor_copy(bsplit[:, 2], bres[:]).then_inc(split_ready, 1)
                    dve.wait_ge(shifted, 48)
                    dve.wait_ge(consts, 4)
                    tt, tsc = nc.vector.tensor_tensor, nc.vector.tensor_scalar
                    link(nc.vector.tensor_copy(dst_i[:, :], cur[:, :]))
                    link(tt(last[:, :], cur[:, :], nxt[:, :], ALU.not_equal))
                    link(tt(cont[:, :], cur[:, :], prv[:, :], ALU.is_equal))
                    link(tsc(notlast[:, :], last[:, :], -1.0, 1.0, ALU.mult, ALU.add))
                    link(tsc(pen[:, :], cont[:, :], -NEVER, NEVER, ALU.mult, ALU.add))
                    link(nc.vector.tensor_tensor_scan(lead[:, :], cont[:, :], zeros[:, :], 1.0, ALU.mult, ALU.add))
                    link(tt(leadend[:, :], lead[:, :], last[:, :], ALU.mult))
                    link(tt(ownlast[:, :], last[:, :], leadend[:, :], ALU.subtract))

                    def masked(flag, value, tile):
                        link(tsc(f1[:, :], value, float(-SKIP), None, ALU.add))
                        link(tt(f1[:, :], f1[:, :], flag, ALU.mult))
                        link(tsc(tile[:, :], f1[:, :], float(SKIP), None, ALU.add))

                    masked(last[:, :], cur[:, :], end_i)
                    masked(ownlast[:, :], cur[:, :], out_i)
                    link(nc.vector.reduce_sum(ends[:, 0:1], leadend[:, :], AX.X))
                    link(tsc(ends[:, 1:2], ends[:, 0:1], -1.0, 1.0, ALU.mult, ALU.add))
                    link(nc.vector.tensor_copy(ends[:, 2:3], lead[:, COLS - 1:COLS]))
                    link(nc.vector.tensor_copy(ends[:, 3:4], cont[:, 0:1]))
                    for j, value in ((0, pos_i), (2, cur)):
                        link(tt(f2[:, :], leadend[:, :], value[:, :], ALU.mult))
                        link(nc.vector.reduce_sum(lead_f[:, j:j + 1], f2[:, :], AX.X))
                    link(tsc(lead_f[:, 1:2], lead_f[:, 0:1], 1.0, None, ALU.mult))
                    link(tsc(lead_f[:, 0:1], lead_f[:, 0:1], float(-N), None, ALU.add))
                    link(tsc(lead_f[:, :], lead_f[:, :], float(-SKIP), ends[:, 0:1], ALU.add, ALU.mult))
                    link(tsc(lead_i[:, :], lead_f[:, :], float(SKIP), None, ALU.add))

                    link(tsc(flagrows[:, 0, :], ends[:, 2:3].broadcast_to([P, R]), -NEVER, NEVER, ALU.mult, ALU.add))
                    link(tsc(flagrows[:, 1, :], ends[:, 3:4].broadcast_to([P, R]), -NEVER, NEVER, ALU.mult, ALU.add))
                    nc.vector.tensor_copy(flagrows[:, 2, :], ends[:, 1:2].broadcast_to([P, R])).then_inc(flags_made, 1)
                    dve.wait_ge(flags_T, 1)
                    for j, k in enumerate(("wpen", "cpen", "noend")):
                        link(nc.vector.tensor_copy(ctile[k][:, :], psT[0][0:R, j * P:(j + 1) * P]))
        with ExitStack() as tmp:
            def ts(name, shape, dt=F32):
                return tmp.enter_context(nc.sbuf_tensor(name, shape, dt))

            mapidx = ts("mapidx", [P, 2, MAPC], I32)
            mapval = ts("mapval", [P, 2, MAPC], I32)
            def carve(first, n):
                part = feats[:, first * NODEC:(first + 2 * n) * NODEC, :].rearrange("p (r c) d -> p r c d", r=2)
                return part, first + 2 * n
            nx, at_ = carve(0, 1)
            na, at_ = carve(at_, 1)
            nb, at_ = carve(at_, 1)
            ncen, at_ = carve(at_, 1)
            njunk, at_ = carve(at_, 1)
            nT, at_ = carve(at_, 1)
            nT = nT.rearrange("p r c d -> p r (c d)")
            nval, at_ = carve(at_, 4)
            nval = nval.rearrange("p r (t c) d -> p r t c d", t=4)
            nsmall = ts("nsmall", [P, 2, 2, NODEC])
            nvar = ts("nvar", [P, 2, NODEC])
            nlnv = ts("nlnv", [P, 2, NODEC])
            nrstd = ts("nrstd", [P, 2, NODEC])
            PAIRS = BLOCKS // 2
            assert BLOCKS % 2 == 1

            class NodeSignal:

                def __init__(self, name, steps):
                    self.sem, self.steps = sem(name), steps

                def at(self, pair, t, par):
                    if isinstance(pair, int) and pair == PAIRS:
                        return PAIRS * 2 * self.steps + t + 1
                    return pair * (2 * self.steps) + (2 * t + par + 1)

                def wait(self, eng, pair, t, par):
                    wait(eng, self.sem, self.at(pair, t, par))

            n_tr, n_ev, n_mm, n_val = (NodeSignal(s, k) for s, k in (("n_tr", 3), ("n_ev", 3), ("n_mm", 3), ("n_val", 4)))
            n_cen, n_sq, n_lv, n_rstd = (NodeSignal(s, 4) for s in ("n_cen", "n_sq", "n_lv", "n_rstd"))
            n_z, n_ez, n_es, n_ln = (NodeSignal(s, 1) for s in ("n_z", "n_ez", "n_es", "n_ln"))
            n_link = sem("n_link")
            nld = [sem("nld_a"), sem("nld_b")]
            nst = [[sem(f"nst{t}_{p}") for p in "ab"] for t in range(4)]
            map_in = [sem("map_in_a"), sem("map_in_b")]
            map_done = [sem("map_done_a"), sem("map_done_b")]
            map_kept = [sem("map_kept_a"), sem("map_kept_b")]
            pool_step = sem("pool_step")

            def block_rows(t, pair, par):
                if isinstance(pair, int) and pair == PAIRS:
                    return t[2 * PAIRS * BLOCK:N, :].rearrange("(p c) d -> p c d", c=NODEC)
                v = t[0:2 * PAIRS * BLOCK, :].rearrange("(b p c) d -> b p (c d)", p=P, c=NODEC)
                return v[bass.ds(2 * pair + par, 1), :, :].rearrange("b p (c d) -> (b p) c d", c=NODEC)

            def over_pairs(eng, body):
                body(0, (0, 1), P)
                with eng.Fori(1, PAIRS) as i:
                    body(i, (0, 1), P)
                body(PAIRS, (0,), TAILP)

            with nc.Block() as block:
                @block.sync
                def _(sp):
                    W1 = MAPH // 2
                    for phase in (0, 1):
                        def ring(i, par):
                            cols = bass.ds((2 * i + par) * MAPC, MAPC)
                            wait(sp, map_done[par], (i + phase * W1) * (16 * MAPC))
                            if phase == 0:
                                sp.dma_start(mapidx[:, par, :], end_i[:, cols]).then_inc(map_in[par], 16)
                                sp.dma_start(mapval[:, par, :], pos_i[:, cols]).then_inc(map_in[par], 16)
                                return
                            if not (isinstance(i, int) and i == 0):
                                sp.dma_start(row_i[:, bass.ds((2 * i + par - 2) * MAPC, MAPC)],
                                             mapval[:, par, :]).then_inc(map_kept[par], 16)
                                wait(sp, map_kept[par], i * 16)
                            sp.dma_start(mapidx[:, par, :], src_i[:, cols]).then_inc(map_in[par], 16)
                        for par in (0, 1):
                            ring(0, par)
                        with sp.Fori(1, W1) as i:
                            ring(i, 0)
                            ring(i, 1)
                    for par in (0, 1):
                        sp.wait_ge(map_done[par], MAPH * 16 * MAPC)
                        j = (MAPH - 2 + par) * MAPC
                        sp.dma_start(row_i[:, j:j + MAPC], mapval[:, par, :]).then_inc(map_kept[par], 16)
                        sp.wait_ge(map_kept[par], W1 * 16)

                @block.gpsimd
                def _(pool):
                    last_node = pool.to_reg(N - 1)
                    W1 = MAPH // 2
                    with pool.Fori(0, W1) as i:
                        for par in (0, 1):
                            pool.wait_ge(map_in[par], i * 32 + 32)
                            pool.sem_inc(pool_step, 1)
                            for j in range(MAPC):
                                nc.gpsimd.indirect_dma_start(
                                    where_d, bass.IndirectOffsetOnAxis(mapidx[:, par, j:j + 1], 0), mapval[:, par, j:j + 1], None,
                                    bounds_check=last_node, oob_is_err=False).then_inc(map_done[par], 16)
                    for par in (0, 1):
                        pool.wait_ge(map_done[par], W1 * 16 * MAPC)
                    with pool.Fori(0, W1) as i:
                        for par in (0, 1):
                            pool.wait_ge(map_in[par], i * 16 + (W1 * 32 + 16))
                            pool.sem_inc(pool_step, 1)
                            for j in range(MAPC):
                                nc.gpsimd.indirect_dma_start(
                                    mapval[:, par, j:j + 1], None, where_d, bass.IndirectOffsetOnAxis(mapidx[:, par, j:j + 1], 0),
                                    bounds_check=last_node, oob_is_err=False).then_inc(map_done[par], 16)

                @block.tensor
                def _(pe):
                    def body(i, pars, parts):
                        for t in range(3):
                            for p in pars:
                                if t == 0:
                                    pe.wait_ge(nld[p], i * 16 + 16)
                                else:
                                    n_val.wait(pe, i, t - 1, p)
                                source = nx[:, p] if t == 0 else nval[:, p, t - 1]
                                for g in range(NODEC // 2):
                                    ins = nc.tensor.transpose(psT[p][:, g * P:(g + 1) * P],
                                                              source[:, 2 * g:2 * g + 2, :].rearrange("p c d -> p (c d)"), ident[:, :])
                                ins.then_inc(n_tr.sem, 1)
                            for p in pars:
                                n_ev.wait(pe, i, t, p)
                                for g in range(NODEC // C):
                                    nc.tensor.matmul(psQ[p][:, g * C * D:(g + 1) * C * D], ones3[:, :], bias3[:, t, 1, :, D:2 * D],
                                                     start=(g == 0), stop=False)
                                for g in range(NODEC // 2):
                                    ins = nc.tensor.matmul(psQ[p][:, g * P:(g + 1) * P], nT[:, p, g * P:(g + 1) * P],
                                                           wqs[:, t, :, D:2 * D], start=False, stop=(g == NODEC // 2 - 1))
                                ins.then_inc(n_mm.sem, 1)
                    over_pairs(pe, body)

                @block.scalar
                def _(act):
                    act.preload_act_table_set("natural_log_exp_and_others")

                    def body(i, pars, parts):
                        for p in pars:
                            wait(act, n_val.sem, i * 8)
                            act.dma_start(nx[0:parts, p, :, :], block_rows(x, i, p)).then_inc(nld[p], 16)
                        for t in range(4):
                            for p in pars:
                                if t < 3:
                                    n_tr.wait(act, i, t, p)
                                    nc.scalar.copy(nT[:, p, :], psT[p][:, :]).then_inc(n_ev.sem, 1)
                            if t == 2:
                                for p in pars:
                                    n_z.wait(act, i, 0, p)
                                    nc.scalar.activation(nb[:, p], na[:, p], ACT.Exp).then_inc(n_ez.sem, 1)
                                for p in pars:
                                    n_es.wait(act, i, 0, p)
                                    nc.scalar.activation(nsmall[:, p, 0, :], nsmall[:, p, 1, :], ACT.Ln).then_inc(n_ln.sem, 1)
                            for p in pars:
                                n_cen.wait(act, i, t, p)
                                for c in range(NODEC):
                                    ins = nc.scalar.activation(njunk[:, p, c, :], ncen[:, p, c, :], ACT.Square, accum_out=nvar[:, p, c:c + 1])
                                ins.then_inc(n_sq.sem, 1)
                                n_sq.wait(act, i, t, p)
                                nc.scalar.activation(nlnv[:, p, :], nvar[:, p, :], ACT.Ln, bias=eps[:, 0:1], scale=1.0 / D).then_inc(n_lv.sem, 1)
                                n_lv.wait(act, i, t, p)
                                nc.scalar.activation(nrstd[:, p, :], nlnv[:, p, :], ACT.Exp, scale=-0.5).then_inc(n_rstd.sem, 1)
                            for p in pars:
                                n_val.wait(act, i, t, p)
                                table = out if t == 3 else rows[t + 1]
                                act.dma_start(block_rows(table, i, p), nval[0:parts, p, t, :, :]).then_inc(nst[t][p], 16)
                    over_pairs(act, body)
                    for t in range(4):
                        for p in (0, 1):
                            act.wait_ge(nst[t][p], 16 * (PAIRS + (p == 0)))

                @block.vector
                def _(dve):
                    LINKS = 14
                    tt, tsc = nc.vector.tensor_tensor, nc.vector.tensor_scalar
                    wide = [P, NODEC, D]

                    def body(i, pars, parts):
                        n = [0]
                        first = i * (2 * LINKS)

                        def link(ins):
                            n[0] += 1
                            ins.then_inc(n_link, 1)
                            dve.wait_ge(n_link, first + n[0])

                        for t in range(4):
                            for p in pars:
                                h = na[:, p]
                                if t < 3:
                                    n_mm.wait(dve, i, t, p)
                                    link(tsc(h, psQ[p][:, :].rearrange("p (c d) -> p c d", d=D), 0.0, None, ALU.max))
                                else:
                                    h = nval[:, p, 2]
                                if t == 2:
                                    m = nsmall[:, p, 0, :]
                                    link(nc.vector.reduce_max(m, h, AX.X))
                                    tt(h, h, m.unsqueeze(2).broadcast_to(wide), ALU.subtract).then_inc(n_z.sem, 1)
                            if t == 2:
                                for p in pars:
                                    n_ez.wait(dve, i, 0, p)
                                    nc.vector.reduce_sum(nsmall[:, p, 1, :], nb[:, p], AX.X).then_inc(n_es.sem, 1)
                            for p in pars:
                                h = na[:, p] if t < 3 else nval[:, p, 2]
                                if t == 2:
                                    n_ln.wait(dve, i, 0, p)
                                    link(tt(nb[:, p], h, nsmall[:, p, 0, :].unsqueeze(2).broadcast_to(wide), ALU.subtract))
                                    link(tt(na[:, p], nb[:, p], nx[:, p], ALU.add))
                                link(nc.vector.reduce_sum(nsmall[:, p, 0, :], h, AX.X))
                                link(tsc(nsmall[:, p, 1, :], nsmall[:, p, 0, :], 1.0 / D, None, ALU.mult))
                                tt(ncen[:, p], h, nsmall[:, p, 1, :].unsqueeze(2).broadcast_to(wide), ALU.subtract).then_inc(n_cen.sem, 1)
                            for p in pars:
                                n_rstd.wait(dve, i, t, p)
                                wait(dve, nst[t][p], i * 16)
                                tt(nval[:, p, t], ncen[:, p], nrstd[:, p, :].unsqueeze(2).broadcast_to(wide), ALU.mult).then_inc(n_val.sem, 1)
                                n_val.wait(dve, i, t, p)
                        assert n[0] == len(pars) * LINKS
                    over_pairs(dve, body)
        chain = {}
        lead_x, xs_ready = signal("lead_x", (1, 2, 3)), signal("xs_ready", (1, 2, 3))
        gathered, gathered_x = landing("gathered", step=16 * C), landing("gathered_x", (0,), 16 * C)
        edges_in, x0_in = landing("edges_in", (0, 1, 2), 32), landing("x0_in", (2,))
        acc_out, skip_out, rows_out = landing("acc_out"), landing("skip_out", (0, 1, 2)), landing("rows_out", (0, 1, 2))
        x0_out, out_done = landing("x0_out", (0,)), landing("out_done", (3,), 16 * C)
        idx_ready, transposed, fT_ready = signal("idx_ready"), signal("transposed"), signal("fT_ready")
        xT_ready, kv_ready, q_ready, qs_ready = signal("xT_ready", (0, 1, 2)), signal("kv_ready"), signal("q_ready"), signal("qs_ready")
        prod_done, alpha_done, floor_done = signal("prod_done"), signal("alpha_done"), signal("floor_done", (3,))
        max_done, dif0_done, dif_ready, exp_ready = (signal(s) for s in ("max_done", "dif0_done", "dif_ready", "exp_ready"))
        sum_done, pv_done, seps_done, sinv_done = signal("sum_done"), signal("pv_done"), signal("seps_done"), signal("sinv_done")
        carried, acc_step = signal("carried", (3,), C), signal("acc_step", step=C)
        norm_done, added, relu_done = signal("norm_done"), signal("added"), signal("relu_done", (0, 1, 2))
        agT_made, agT_ready, wo_ready = signal("agT_made", (3,)), signal("agT_ready", (3,)), signal("wo_ready", (3,))
        hmax_done, z_ready, ez_ready, esum_ready = (signal(s, (2,)) for s in ("hmax_done", "z_ready", "ez_ready", "esum_ready"))
        ln_ready, lsm_done, res_done = (signal(s, (2,)) for s in ("ln_ready", "lsm_done", "res_done"))
        res_ready = signal("res_ready", (3,))
        fsum_done, mean_done, cen_ready, rmask_done = (signal(s) for s in ("fsum_done", "mean_done", "cen_ready", "rmask_done"))
        square_done, lnv_done, rstd_ready, value_ready = (signal(s) for s in ("square_done", "lnv_done", "rstd_ready", "value_ready"))
        oidx_ready = signal("oidx_ready", (3,))
        fix_preset, fix_ready, fix_in, fix_out = event("fix_preset"), event("fix_ready"), sem("fix_in"), event("fix_out", step=16)
        ends_ready, ends_T, tot_ready, tot_T = (event(s) for s in ("ends_ready", "ends_T", "tot_ready", "tot_T"))
        w_ready, w_exp, m_ready, m_exp = (event(s) for s in ("w_ready", "w_exp", "m_ready", "m_exp"))
        f_agg, f_aggT, f_aggTs, f_wo = (event(s, (3,)) for s in ("f_agg", "f_aggT", "f_aggTs", "f_wo"))
        f_z, f_ez, f_es, f_ln = (event(s, (2,)) for s in ("f_z", "f_ez", "f_es", "f_ln"))
        f_cen, f_sq, f_lv, f_rstd = (event(s) for s in ("f_cen", "f_sq", "f_lv", "f_rstd"))
        fix_T, init_ready, init_T = (event(s, (0, 1, 2)) for s in ("fix_T", "init_ready", "init_T"))
        c_link, s_link = sem("c_link"), sem("s_link")

        def at(e, l):
            return e.at(l, 0)

        big = sb("big", [P, NH, COLS])
        cG, cA, cR = sb("cG", [R, P + 1]), sb("cA", [R, P + 1]), sb("cR", [D, P + 1])
        rm, ra, rmF, rf, rt = (sb("r_" + s, [P, R]) for s in ("m", "a", "mF", "f", "t"))
        rx = sb("rx", [P, 2, D])
        fa, fb, fc, fcen = (sb("f_" + s, [P, D]) for s in ("a", "b", "c", "cen"))
        faggT = sb("f_T", [D, P])
        fsm = sb("fsm", [P, 8])
        init = sb("init", [P, D])

        for l in LAYERS:
            H = NH if l == 3 else 1
            F = D // H
            RL = D + H
            SCALE = float(F) ** -0.5
            lag = 3 if l > 1 else 2
            G = 2 * D if l < 3 else D

            def heads(tile, n=C):
                return tile[:, 0:H * n].rearrange("p (h c) -> p h c", h=H)

            def over_features(small):
                return small.rearrange("p h c -> p c h").unsqueeze(3).broadcast_to([P, C, H, F])

            def split(t):
                return t.rearrange("p c (h f) -> p c h f", h=H)

            def wide(small):
                return small.unsqueeze(2).broadcast_to([P, C, D])

            def link_from(eng, semaphore, start):
                n = [start]

                def link(ins):
                    n[0] += 1
                    ins.then_inc(semaphore, 1)
                    eng.wait_ge(semaphore, n[0])
                return link, n

            with nc.Block() as block:
                @block.sync
                def _(sp):
                    def load(h):
                        after(sp, transposed, l, h.plus(-2))
                        for lo, hi, t in ((0, SPLIT, edge_attr[0:SPLIT * COLS, :]), (SPLIT, P, etail_d)):
                            e = t.rearrange("(p j) d -> p j d", j=COLS)
                            sp.dma_start(T[lo:hi, h.par, :, 1, :], e[:, h.cols(), :]).then_inc(edges_in.sem[h.par], 16)

                    def load_x0(h):
                        after(sp, res_done, l, h.plus(-2))
                        sp.dma_start(x0[:, h.par, :, :], by_edge(x0_d)[:, h.cols(), :]).then_inc(x0_in.sem[h.par], 16)

                    def keep(h):
                        landed(sp, gathered_x, l, h)
                        sp.dma_start(by_edge(x0_d)[:, h.cols(), :], xs[:, h.par, :, :]).then_inc(x0_out.sem[h.par], 16)

                    def store(h):
                        if l < 3:
                            after(sp, qs_ready, l, h)
                            sp.dma_start(by_edge(skip_d)[:, h.cols(), :], qs[:, h.par, :, D:2 * D]).then_inc(skip_out.sem[h.par], 16)
                        after(sp, acc_step, l, h)
                        sp.dma_start(by_edge(acc_d)[:, h.cols(), :], acc[:, h.par * C:(h.par + 1) * C, :]).then_inc(acc_out.sem[h.par], 16)

                    def store_value(h):
                        after(sp, value_ready, l, h)
                        sp.dma_start(by_edge(rows[l + 1][N:N + EP, :])[:, h.cols(), :], feats[:, h.cols(), :]).then_inc(rows_out.sem[h.par], 16)

                    def step(h):
                        if l < 3:
                            stage(load, h, 2, HALVES)
                        if l == 2:
                            stage(load_x0, h, 0, HALVES)
                        if l == 0:
                            stage(keep, h, 1, HALVES)
                        stage(store, h, -1, HALVES)
                        if l < 3:
                            stage(store_value, h, -lag, HALVES)
                    run(sp, HALVES, step, -2, HALVES + lag - 1)
                    for landing_ in (acc_out, skip_out, rows_out, x0_out):
                        if l in landing_.layers:
                            for p in (0, 1):
                                landed(sp, landing_, l, Half(HALVES // 2 - 1, p))

                @block.gpsimd
                def _(pool):
                    bound = pool.to_reg(N - 1 if l == 0 else N + EP - 1)
                    last_node = pool.to_reg(N - 1)
                    last_pos = pool.to_reg(EP - 1)
                    last_row = pool.to_reg(N + EP - 1)

                    def gather_rows(tile, table, index, bnd, semaphore):
                        nc.gpsimd.indirect_dma_start(tile, None, table, bass.IndirectOffsetOnAxis(index, 0),
                                                     bounds_check=bnd, oob_is_err=False).then_inc(semaphore, 16)

                    def scatter_rows(table, index, tile, bnd, semaphore):
                        nc.gpsimd.indirect_dma_start(table, bass.IndirectOffsetOnAxis(index, 0), tile, None,
                                                     bounds_check=bnd, oob_is_err=False).then_inc(semaphore, 16)

                    def gather(h):
                        after(pool, transposed, l, h.plus(-2))
                        after(pool, idx_ready, l, h)
                        if l == 0:
                            landed(pool, x0_out, l, h.plus(-2))
                        pool.sem_inc(pool_step, 1)
                        for c in range(C):
                            gather_rows(T[:, h.par, c, 0, :] if l < 3 else T3[:, h.par, c, :], rows[l], idxr[:, h.par, 0, c:c + 1], bound, gathered.sem[h.par])
                            if l == 0:
                                gather_rows(xs[:, h.par, c, :], rows[0], idxr[:, h.par, 1, c:c + 1], bound, gathered_x.sem[h.par])

                    def scatter(h):
                        after(pool, oidx_ready, l, h)
                        after(pool, value_ready, l, h)
                        pool.sem_inc(pool_step, 1)
                        for c in range(C):
                            scatter_rows(out, oidx[:, h.par, c:c + 1], yout[:, h.par, c, :], last_node, out_done.sem[h.par])

                    def step(h):
                        stage(gather, h, 2, HALVES)
                        if l == 3:
                            stage(scatter, h, -lag, HALVES)
                    run(pool, HALVES, step, -2, HALVES + lag - 1)
                    for p in (0, 1):
                        for landing_ in (acc_out, skip_out, out_done, rows_out):
                            if l in landing_.layers:
                                landed(pool, landing_, l, Half(HALVES // 2 - 1, p))
                    pool.wait_ge(fix_preset.sem, at(fix_preset, l))
                    pool.sem_inc(pool_step, 1)
                    gather_rows(rf[:, 0:D], acc_d, lead_i[:, 0:1], last_pos, fix_in)
                    if l < 3:
                        gather_rows(rx[:, 0, :], skip_d, lead_i[:, 0:1], last_pos, fix_in)
                        gather_rows(rx[:, 1, :], x0_d, lead_i[:, 0:1], last_pos, fix_in)
                    pool.wait_ge(fix_ready.sem, at(fix_ready, l))
                    pool.sem_inc(pool_step, 1)
                    if l < 3:
                        scatter_rows(rows[l + 1], lead_i[:, 1:2], fix[:, :], last_row, fix_out.sem)
                    else:
                        scatter_rows(out, lead_i[:, 2:3], fix[:, :], last_node, fix_out.sem)
                    pool.wait_ge(fix_out.sem, at(fix_out, l))

                @block.tensor
                def _(pe):
                    def transposes(h):
                        p = h.par
                        landed(pe, gathered, l, h)
                        if l < 3:
                            landed(pe, edges_in, l, h)
                        if l == 0:
                            landed(pe, gathered_x, l, h)
                        else:
                            after(pe, xs_ready, l, h)
                        after(pe, fT_ready, l, h.plus(-2))
                        if l < 3:
                            after(pe, xT_ready, l, h.plus(-2))
                            for c in range(C):
                                nc.tensor.transpose(psT[p][:, c * P:(c + 1) * P], T[:, p, c, :, :].rearrange("p t d -> p (t d)"), ident[:, :])
                        else:
                            for g in range(2):
                                nc.tensor.transpose(psT[p][:, g * P:(g + 1) * P],
                                                    T3[:, p, 2 * g:2 * g + 2, :].rearrange("p c d -> p (c d)"), ident[:, :])
                        for g in range(2):
                            o = psX[p][:, g * P:(g + 1) * P] if l < 3 else psT[p][:, (2 + g) * P:(3 + g) * P]
                            ins = nc.tensor.transpose(o, xs[:, p, 2 * g:2 * g + 2, :].rearrange("p c d -> p (c d)"), ident[:, :])
                        ins.then_inc(transposed.sem, 1)

                    def products(h):
                        p = h.par
                        after(pe, prod_done, l, h.plus(-2))
                        after(pe, pv_done, l, h.plus(-2))
                        after(pe, fT_ready, l, h)
                        if l < 3:
                            nc.tensor.matmul(psKV[p][:, :], ones3[:, :], bias3[:, l, 0, :, :], start=True, stop=False)
                            for c in range(C):
                                ins = nc.tensor.matmul(psKV[p][:, c * P:(c + 1) * P], fT[:, p, c * P:(c + 1) * P], wkv[:, l, :],
                                                       start=False, stop=(c == C - 1))
                        else:
                            for g in range(2):
                                ins = nc.tensor.matmul(psKV[p][:, g * 2 * P:(g + 1) * 2 * P], fT[:, p, g * P:(g + 1) * P], wkv1[:, :, :],
                                                       start=True, stop=True)
                        ins.then_inc(kv_ready.sem, 1)
                        after(pe, qs_ready, l, h.plus(-2))
                        if l < 3:
                            after(pe, xT_ready, l, h)
                            nc.tensor.matmul(psQ[p][:, :], ones3[:, :], bias3[:, l, 1, :, :], start=True, stop=False)
                        for g in range(2):
                            w = xT[:, p, g * P:(g + 1) * P] if l < 3 else fT[:, p, (2 + g) * P:(3 + g) * P]
                            ins = nc.tensor.matmul(psQ[p][:, g * 2 * G:(g + 1) * 2 * G], w, wqs[:, l, :, :] if l < 3 else wq1[:, :, :],
                                                   start=(l == 3), stop=(l == 3 or g == 1))
                        ins.then_inc(q_ready.sem, 1)

                    def agg_turned(h):
                        after(pe, norm_done, l, h)
                        after(pe, agT_ready, l, h.plus(-1))
                        for g in range(2):
                            ins = nc.tensor.transpose(psX[0][:, g * P:(g + 1) * P],
                                                      t1[:, 2 * g:2 * g + 2, :].rearrange("p c d -> p (c d)"), ident[:, :])
                        ins.then_inc(agT_made.sem, 1)

                    def agg_product(h):
                        after(pe, agT_ready, l, h)
                        after(pe, added, l, h.plus(-1))
                        for g in range(2):
                            ins = nc.tensor.matmul(psX[1][:, g * P:(g + 1) * P], agT[:, g * P:(g + 1) * P], wo1[:, :, :],
                                                   start=True, stop=True)
                        ins.then_inc(wo_ready.sem, 1)

                    def step(h):
                        stage(products, h, 0, HALVES)
                        if l == 3:
                            stage(agg_turned, h, -2, HALVES)
                        stage(transposes, h, 1, HALVES)
                        if l == 3:
                            stage(agg_product, h, -2, HALVES)
                    run(pe, HALVES, step, -1, HALVES + 1)
                    pe.wait_ge(ends_ready.sem, at(ends_ready, l))
                    for j, t in enumerate((rm, ra, rmF, rf)):
                        ins = nc.tensor.transpose(psT[0][0:RL, j * P:(j + 1) * P], t[:, 0:RL], ident[:, :])
                    ins.then_inc(ends_T.sem, 1)
                    pe.wait_ge(tot_ready.sem, at(tot_ready, l))
                    nc.tensor.transpose(psT[1][:, 0:RL], ctile["t"][0:RL, :], ident[0:RL, 0:RL]).then_inc(tot_T.sem, 1)
                    if l == 3:
                        pe.wait_ge(f_agg.sem, at(f_agg, l))
                        nc.tensor.transpose(psX[0][0:D, 0:P], fa[:, :], ident[:, :]).then_inc(f_aggT.sem, 1)
                        pe.wait_ge(f_aggTs.sem, at(f_aggTs, l))
                        nc.tensor.matmul(psX[1][:, 0:D], faggT[0:D, :], wo1[0:D, 0, :], start=True, stop=True).then_inc(f_wo.sem, 1)
                    else:
                        pe.wait_ge(fix_ready.sem, at(fix_ready, l))
                        nc.tensor.transpose(psX[0][0:D, 0:P], fix[:, :], ident[:, :]).then_inc(fix_T.sem, 1)
                        pe.wait_ge(init_ready.sem, at(init_ready, l))
                        nc.tensor.transpose(psX[1][:, 0:D], cR[0:D, 1:P + 1], ident[0:D, 0:D]).then_inc(init_T.sem, 1)

                @block.scalar
                def _(act):
                    def evacuate(h):
                        p = h.par
                        after(act, transposed, l, h)
                        after(act, kv_ready, l, h.plus(-2))
                        after(act, q_ready, l, h.plus(-2))
                        nc.scalar.copy(fT[:, p, :], psT[p][:, :]).then_inc(fT_ready.sem, 1)
                        if l < 3:
                            nc.scalar.copy(xT[:, p, :], psX[p][:, 0:2 * P]).then_inc(xT_ready.sem, 1)

                    def indices(h):
                        p = h.par
                        landed(act, gathered, l, h.plus(-2))
                        if l == 0:
                            landed(act, gathered_x, l, h.plus(-2))
                            nc.scalar.copy(idxr[:, p, 1, :], dst_i[:, h.cols()])
                        nc.scalar.copy(idxr[:, p, 0, :], (src_i if l == 0 else row_i)[:, h.cols()]).then_inc(idx_ready.sem, 1)

                    def queries(h):
                        p = h.par
                        after(act, q_ready, l, h)
                        after(act, added if l < 3 else prod_done, l, h.plus(-2))
                        if l < 3:
                            landed(act, skip_out, l, h.plus(-2))
                        nc.scalar.copy(qs[:, p, :, 0:G], psQ[p][:, 0:C * G].rearrange("p (c d) -> p c d", c=C)).then_inc(qs_ready.sem, 1)

                    def residual(h):
                        after(act, xs_ready, l, h)
                        after(act, added, l, h.plus(-2))
                        nc.scalar.copy(x0[:, h.par, :, :], xs[:, h.par, :, :]).then_inc(res_ready.sem, 1)

                    def variance(h):
                        p = h.par
                        after(act, cen_ready, l, h)
                        after(act, value_ready, l, h.plus(-2))
                        for c in range(C):
                            ins = nc.scalar.activation(junk[:, c, :], cen[:, p, c, :], ACT.Square, accum_out=var[:, p, c:c + 1])
                        ins.then_inc(square_done.sem, 1)
                        after(act, square_done, l, h)
                        nc.scalar.activation(lnv[:, :], var[:, p, :], ACT.Ln, bias=eps[:, 0:1], scale=1.0 / D).then_inc(lnv_done.sem, 1)
                        after(act, lnv_done, l, h)
                        nc.scalar.activation(rstd[:, p, :], lnv[:, :], ACT.Exp, scale=-0.5).then_inc(rstd_ready.sem, 1)

                    def exponentials(h):
                        p = h.par
                        after(act, dif_ready, l, h)
                        after(act, acc_step, l, h.plus(-2))
                        nc.scalar.activation(ex[:, p, :, 0:H * C], dif[:, p, :, 0:H * C], ACT.Exp, scale=SCALE).then_inc(exp_ready.sem, 1)

                    def aggregate(h):
                        after(act, agT_made, l, h)
                        after(act, wo_ready, l, h.plus(-1))
                        nc.scalar.copy(agT[:, :], psX[0][:, 0:2 * P]).then_inc(agT_ready.sem, 1)

                    def softmax_exp(h):
                        after(act, z_ready, l, h)
                        nc.scalar.activation(ez[:, :, :], t1[:, :, :], ACT.Exp).then_inc(ez_ready.sem, 1)

                    def logarithm(h):
                        after(act, esum_ready, l, h)
                        nc.scalar.activation(lns[:, :], esum[:, :], ACT.Ln).then_inc(ln_ready.sem, 1)

                    def step(h):
                        stage(queries, h, 0, HALVES)
                        if l == 3:
                            stage(aggregate, h, -2, HALVES)
                        stage(evacuate, h, 1, HALVES)
                        stage(indices, h, 3, HALVES)
                        if l == 2:
                            stage(logarithm, h, -2, HALVES)
                        stage(variance, h, -lag, HALVES)
                        stage(exponentials, h, 0, HALVES)
                        if l == 2:
                            stage(softmax_exp, h, -1, HALVES)
                        if l == 3:
                            stage(residual, h, 0, HALVES)
                    act.preload_act_table_set("natural_log_exp_and_others")
                    run(act, HALVES, step, -3, HALVES + lag - 1)
                    link, n = link_from(act, s_link, chain.get("act", 0))
                    act.wait_ge(w_ready.sem, at(w_ready, l))
                    link(nc.scalar.activation(ctile["e1"][0:RL, :], ctile["d1"][0:RL, :], ACT.Exp, scale=SCALE))
                    nc.scalar.activation(ctile["e2"][0:RL, :], ctile["d2"][0:RL, :], ACT.Exp, scale=SCALE).then_inc(w_exp.sem, 1)
                    act.wait_ge(m_ready.sem, at(m_ready, l))
                    link(nc.scalar.activation(ctile["e1"][0:RL, :], ctile["d1"][0:RL, :], ACT.Exp, scale=SCALE))
                    nc.scalar.activation(ctile["e2"][0:RL, :], ctile["d2"][0:RL, :], ACT.Exp, scale=SCALE).then_inc(m_exp.sem, 1)
                    if l == 2:
                        act.wait_ge(f_z.sem, at(f_z, l))
                        nc.scalar.activation(fc[:, :], fa[:, :], ACT.Exp).then_inc(f_ez.sem, 1)
                        act.wait_ge(f_es.sem, at(f_es, l))
                        nc.scalar.activation(fsm[:, 1:2], fsm[:, 0:1], ACT.Ln).then_inc(f_ln.sem, 1)
                    act.wait_ge(f_cen.sem, at(f_cen, l))
                    nc.scalar.activation(fc[:, :], fcen[:, :], ACT.Square, accum_out=fsm[:, 4:5]).then_inc(f_sq.sem, 1)
                    act.wait_ge(f_sq.sem, at(f_sq, l))
                    nc.scalar.activation(fsm[:, 5:6], fsm[:, 4:5], ACT.Ln, bias=eps[:, 0:1], scale=1.0 / D).then_inc(f_lv.sem, 1)
                    act.wait_ge(f_lv.sem, at(f_lv, l))
                    nc.scalar.activation(fsm[:, 6:7], fsm[:, 5:6], ACT.Exp, scale=-0.5).then_inc(f_rstd.sem, 1)
                    chain["act"] = n[0]

                @block.vector
                def _(dve):
                    tt, tsc = nc.vector.tensor_tensor, nc.vector.tensor_scalar

                    def kv_of(h):
                        return psKV[h.par][:, :].rearrange("p (c d) -> p c d", c=C)

                    def lead_part(h):
                        after(dve, xs_ready, l, h.plus(-1))
                        tt(leadx[:, :, :], wide(lead[:, h.cols()]), fix[:, :].unsqueeze(1).broadcast_to([P, C, D]), ALU.mult).then_inc(lead_x.sem, 1)

                    def inputs(h):
                        after(dve, transposed, l, h.plus(-2))
                        if l == 3:
                            after(dve, res_ready, l, h.plus(-2))
                        after(dve, lead_x, l, h)
                        tt(xs[:, h.par, :, :], leadx[:, :, :], feats[:, h.cols(), :], ALU.add).then_inc(xs_ready.sem, 1)

                    def qk_product(h):
                        after(dve, kv_ready, l, h)
                        after(dve, qs_ready, l, h)
                        tt(prod[:, :, :], kv_of(h)[:, :, 0:D], qs[:, h.par, :, 0:D], ALU.mult).then_inc(prod_done.sem, 1)

                    def scores(h):
                        after(dve, prod_done, l, h)
                        nc.vector.reduce_sum(heads(alpha[:, h.par, :]).rearrange("p h c -> p c h"), split(prod[:, :, :]), AX.X).then_inc(alpha_done.sem, 1)

                    def maxima(h):
                        j, am = h.k * C, heads(alpha[:, h.par, :])
                        after(dve, alpha_done, l, h)
                        if l == 3:
                            am = heads(alphac[:, :])
                            tsc(am, heads(alpha[:, h.par, :]), -1.0e9 / SCALE, None, ALU.max).then_inc(floor_done.sem, 1)
                            after(dve, floor_done, l, h)
                        for hd in range(H):
                            ins = nc.vector.tensor_tensor_scan(M[:, hd, bass.ds(j + 1, C)], pen[:, h.cols()], am[:, hd, :],
                                                               M[:, hd, bass.ds(j, 1)], ALU.add, ALU.max)
                        ins.then_inc(max_done.sem, 1)

                    def decays(h):
                        after(dve, max_done, l, h)
                        after(dve, dif_ready, l, h.plus(-1))
                        tt(heads(dif0[:, :]), M[:, 0:H, bass.ds(h.k * C, C)], pen[:, h.cols()].unsqueeze(1).broadcast_to([P, H, C]),
                           ALU.add).then_inc(dif0_done.sem, 1)

                    def exponents(h):
                        p, m = h.par, M[:, 0:H, bass.ds(h.k * C + 1, C)]
                        after(dve, exp_ready, l, h.plus(-2))
                        after(dve, dif0_done, l, h)
                        tt(heads(dif[:, p, 0, :]), heads(dif0[:, :]), m, ALU.subtract)
                        tt(heads(dif[:, p, 1, :]), heads(alpha[:, p, :]), m, ALU.subtract).then_inc(dif_ready.sem, 1)

                    def totals(h):
                        p, j = h.par, h.k * C
                        decay, weight = heads(ex[:, p, 0, :]), heads(ex[:, p, 1, :])
                        after(dve, exp_ready, l, h)
                        for hd in range(H):
                            ins = nc.vector.tensor_tensor_scan(S[:, hd, bass.ds(j + 1, C)], decay[:, hd, :], weight[:, hd, :],
                                                               S[:, hd, bass.ds(j, 1)], ALU.mult, ALU.add)
                        ins.then_inc(sum_done.sem, 1)

                    def weighted(h):
                        after(dve, exp_ready, l, h)
                        after(dve, acc_step, l, h.plus(-1))
                        tt(split(pv[:, :, :]), split(kv_of(h)[:, :, D:2 * D]), over_features(heads(ex[:, h.par, 1, :])), ALU.mult).then_inc(pv_done.sem, 1)

                    def accumulate(c):
                        def piece(h):
                            p, decay = h.par, heads(ex[:, h.par, 0, :])
                            before = acc[:, (p * C + c - 1) % (2 * C), :]
                            if c == 0:
                                after(dve, pv_done, l, h)
                                landed(dve, acc_out, l, h.plus(-2))
                            wait(dve, acc_step.sem, acc_step.at(l, h.k, c))
                            if l < 3:
                                ins = nc.vector.scalar_tensor_tensor(acc[:, p * C + c, :], before, decay[:, 0, c:c + 1], pv[:, c, :],
                                                                     ALU.mult, ALU.add)
                            else:
                                tt(carry[:, :].rearrange("p (h f) -> p h f", h=H), before.rearrange("p (h f) -> p h f", h=H),
                                   decay[:, :, c:c + 1].broadcast_to([P, H, F]), ALU.mult).then_inc(carried.sem, 1)
                                wait(dve, carried.sem, carried.at(l, h.k, c + 1))
                                ins = tt(acc[:, p * C + c, :], carry[:, :], pv[:, c, :], ALU.add)
                            ins.then_inc(acc_step.sem, 1)
                        return piece

                    acc0, acc1, acc2, acc3 = (accumulate(c) for c in range(C))

                    def divisors(h):
                        after(dve, sum_done, l, h)
                        after(dve, sinv_done, l, h.plus(-1))
                        tsc(heads(stot[:, :]), S[:, 0:H, bass.ds(h.k * C + 1, C)], 1.0e-9 if l == 3 else 0.0, None, ALU.add).then_inc(seps_done.sem, 1)

                    def inverses(h):
                        after(dve, norm_done, l, h.plus(-1))
                        after(dve, seps_done, l, h)
                        nc.vector.reciprocal(heads(sinv[:, :]), heads(stot[:, :])).then_inc(sinv_done.sem, 1)

                    def aggregates(h):
                        p = h.par
                        after(dve, sinv_done, l, h)
                        after(dve, acc_step, l, h)
                        if l == 3:
                            after(dve, agT_made, l, h.plus(-1))
                        tt(split(t1[:, :, :]), split(acc[:, p * C:(p + 1) * C, :]), over_features(heads(sinv[:, :])), ALU.mult).then_inc(norm_done.sem, 1)

                    def skip_added(h):
                        if l < 3:
                            after(dve, norm_done, l, h)
                            tt(t2[:, :, :], t1[:, :, :], qs[:, h.par, :, D:2 * D], ALU.add).then_inc(added.sem, 1)
                        else:
                            after(dve, wo_ready, l, h)
                            after(dve, res_ready, l, h)
                            tt(t3[:, :, :], psX[1][:, 0:C * D].rearrange("p (c d) -> p c d", c=C), x0[:, h.par, :, :], ALU.add).then_inc(added.sem, 1)

                    def relu(h):
                        after(dve, added, l, h)
                        tsc(t3[:, :, :], t2[:, :, :], 0.0, None, ALU.max).then_inc(relu_done.sem, 1)

                    def shifted_max(h):
                        after(dve, relu_done, l, h)
                        nc.vector.reduce_max(hmax[:, :], t3[:, :, :], AX.X).then_inc(hmax_done.sem, 1)
                        after(dve, hmax_done, l, h)
                        tt(t1[:, :, :], t3[:, :, :], wide(hmax[:, :]), ALU.subtract).then_inc(z_ready.sem, 1)

                    def exp_sum(h):
                        after(dve, ez_ready, l, h)
                        nc.vector.reduce_sum(esum[:, :], ez[:, :, :], AX.X).then_inc(esum_ready.sem, 1)

                    def log_added(h):
                        after(dve, ln_ready, l, h)
                        tt(t2[:, :, :], t1[:, :, :], wide(lns[:, :]), ALU.subtract).then_inc(lsm_done.sem, 1)
                        after(dve, lsm_done, l, h)
                        landed(dve, x0_in, l, h)
                        tt(t3[:, :, :], t2[:, :, :], x0[:, h.par, :, :], ALU.add).then_inc(res_done.sem, 1)

                    def row_sums(h):
                        after(dve, (relu_done, relu_done, res_done, added)[l], l, h)
                        nc.vector.reduce_sum(csum[:, :], t3[:, :, :], AX.X).then_inc(fsum_done.sem, 1)

                    def means(h):
                        after(dve, fsum_done, l, h)
                        tsc(mean[:, :], csum[:, :], 1.0 / D, None, ALU.mult).then_inc(mean_done.sem, 1)

                    def centred(h):
                        after(dve, mean_done, l, h)
                        after(dve, value_ready, l, h.plus(-2))
                        tt(cen[:, h.par, :, :], t3[:, :, :], wide(mean[:, :]), ALU.subtract).then_inc(cen_ready.sem, 1)

                    def row_scales(h):
                        after(dve, rstd_ready, l, h)
                        after(dve, value_ready, l, h.plus(-1))
                        tt(rmask[:, :], rstd[:, h.par, :], ownlast[:, h.cols()], ALU.mult).then_inc(rmask_done.sem, 1)

                    def values(h):
                        p = h.par
                        after(dve, rmask_done, l, h)
                        if l == 3:
                            landed(dve, out_done, l, h.plus(-2))
                            nc.vector.tensor_copy(oidx[:, p, :], out_i[:, h.cols()]).then_inc(oidx_ready.sem, 1)
                        target = feats[:, h.cols(), :] if l < 3 else yout[:, p, :, :]
                        tt(target, cen[:, p, :, :], wide(rmask[:, :]), ALU.mult).then_inc(value_ready.sem, 1)

                    pieces = [(weighted, -1), (qk_product, 0), (totals, -1), (acc0, -1), (scores, 0), (acc1, -1), (maxima, 0),
                              (acc2, -1), (decays, 0), (acc3, -1), (exponents, 0)]
                    if l < 2:
                        x_at_dst = [(lead_part, 2), (inputs, 2)] if l > 0 else [(None, 0), (None, 0)]
                        pieces += [(divisors, -1), (row_scales, -2), (inverses, -1), (values, -2), (aggregates, -1), x_at_dst[0],
                                   (skip_added, -1), x_at_dst[1], (relu, -1), (row_sums, -1), (means, -1), (centred, -1)]
                    elif l == 2:
                        pieces += [(divisors, -1), (exp_sum, -2), (row_scales, -3), (inverses, -1), (values, -3), (log_added, -2),
                                   (lead_part, 2), (row_sums, -2), (inputs, 2), (means, -2), (centred, -2), (aggregates, -1),
                                   (skip_added, -1), (relu, -1), (shifted_max, -1)]
                    else:
                        pieces += [(divisors, -1), (row_scales, -3), (inverses, -1), (values, -3), (skip_added, -2), (aggregates, -1),
                                   (row_sums, -2), (lead_part, 2), (means, -2), (inputs, 2), (centred, -2)]
                    pieces = [(piece, off) for piece, off in pieces if piece]

                    def step(h):
                        for piece, off in pieces:
                            stage(piece, h, off, HALVES)
                    run(dve, HALVES, step, -2, HALVES + lag - 1)

                    link, n = link_from(dve, c_link, chain.get("dve", 0))
                    after(dve, value_ready, l, Half(HALVES // 2 - 1, 1))
                    after(dve, max_done, l, Half(HALVES // 2 - 1, 1))
                    lm = leadend[:, :].unsqueeze(1).broadcast_to([P, H, COLS])
                    link(tt(big[:, 0:H, :], M[:, 0:H, 1:COLS + 1], lm, ALU.mult))
                    link(nc.vector.reduce_sum(fsm[:, 0:H], big[:, 0:H, :], AX.X))
                    hb = [P, H, F]

                    def spread(tile, small):
                        link(nc.vector.tensor_copy(tile[:, 0:D].rearrange("p (h f) -> p h f", h=H), small.unsqueeze(2).broadcast_to(hb)))
                        link(nc.vector.tensor_copy(tile[:, D:RL], small))
                    spread(rmF, fsm[:, 0:H])
                    link(nc.vector.tensor_copy(fsm[:, 4:4 + H], M[:, 0:H, COLS:COLS + 1].rearrange("p h o -> p (h o)")))
                    spread(rm, fsm[:, 4:4 + H])
                    link(tt(big[:, 0:H, :], S[:, 0:H, 1:COLS + 1], lm, ALU.mult))
                    link(nc.vector.memset(rf[:, :], 0.0))
                    link(nc.vector.memset(rx[:, :, :], 0.0))
                    nc.vector.reduce_sum(rf[:, D:RL], big[:, 0:H, :], AX.X).then_inc(fix_preset.sem, 1)
                    dve.wait_ge(fix_preset.sem, at(fix_preset, l))
                    link(nc.vector.tensor_copy(ra[:, 0:D], acc[:, 2 * C - 1, :]))
                    link(nc.vector.tensor_copy(ra[:, D:RL], S[:, 0:H, COLS:COLS + 1].rearrange("p h o -> p (h o)")))
                    dve.wait_ge(fix_in, 48 * (l + 1) if l < 3 else 48 * 3 + 16)
                    nc.vector.tensor_copy(fsm[:, 0:1], ends[:, 0:1]).then_inc(ends_ready.sem, 1)
                    dve.wait_ge(ends_T.sem, at(ends_T, l))
                    c = {k: v[0:RL, :] for k, v in ctile.items()}
                    for j, k in enumerate(("m", "a", "mF", "f")):
                        link(nc.vector.tensor_copy(c[k], psT[0][0:RL, j * P:(j + 1) * P]))
                    link(nc.vector.memset(cG[:, 0:1], NEVER))
                    link(nc.vector.memset(cA[:, 0:1], 0.0))
                    g0, g1 = cG[0:RL, 0:P], cG[0:RL, 1:P + 1]
                    link(nc.vector.tensor_tensor_scan(g1, c["wpen"], c["m"], NEVER, ALU.add, ALU.max))
                    link(tt(c["t"], g0, c["wpen"], ALU.add))
                    link(tt(c["d1"], c["t"], g1, ALU.subtract))
                    tt(c["d2"], c["m"], g1, ALU.subtract).then_inc(w_ready.sem, 1)
                    dve.wait_ge(w_exp.sem, at(w_exp, l))
                    link(tt(c["t"], c["e2"], c["a"], ALU.mult))
                    link(nc.vector.tensor_tensor_scan(cA[0:RL, 1:P + 1], c["e1"], c["t"], 0.0, ALU.mult, ALU.add))
                    link(tt(c["a"], g0, c["cpen"], ALU.add))
                    link(tt(c["t"], c["a"], c["mF"], ALU.max))
                    link(tt(c["d1"], c["a"], c["t"], ALU.subtract))
                    tt(c["d2"], c["mF"], c["t"], ALU.subtract).then_inc(m_ready.sem, 1)
                    dve.wait_ge(m_exp.sem, at(m_exp, l))
                    link(tt(c["a"], cA[0:RL, 0:P], c["e1"], ALU.mult))
                    link(tt(c["m"], c["f"], c["e2"], ALU.mult))
                    tt(c["t"], c["a"], c["m"], ALU.add).then_inc(tot_ready.sem, 1)
                    dve.wait_ge(tot_T.sem, at(tot_T, l))
                    link(tsc(fsm[:, 0:H], psT[1][:, D:RL], ends[:, 1:2], 1.0e-9 if l == 3 else None, ALU.add,
                             *([ALU.add] if l == 3 else [])))
                    link(nc.vector.reciprocal(fsm[:, 4:4 + H], fsm[:, 0:H]))
                    link(tt(fb[:, :].rearrange("p (h f) -> p h f", h=H), psT[1][:, 0:D].rearrange("p (h f) -> p h f", h=H),
                            fsm[:, 4:4 + H].unsqueeze(2).broadcast_to(hb), ALU.mult))
                    if l < 3:
                        link(tt(fc[:, :], fb[:, :], rx[:, 0, :], ALU.add))
                        link(tsc(fb[:, :], fc[:, :], 0.0, None, ALU.max))
                    else:
                        nc.vector.tensor_copy(fa[:, :], fb[:, :]).then_inc(f_agg.sem, 1)
                        dve.wait_ge(f_aggT.sem, at(f_aggT, l))
                        nc.vector.tensor_copy(faggT[0:D, :], psX[0][0:D, 0:P]).then_inc(f_aggTs.sem, 1)
                        dve.wait_ge(f_wo.sem, at(f_wo, l))
                        link(tt(fb[:, :], psX[1][:, 0:D], fix[:, :], ALU.add))
                    if l == 2:
                        link(nc.vector.reduce_max(fsm[:, 0:1], fb[:, :], AX.X))
                        tsc(fa[:, :], fb[:, :], fsm[:, 0:1], None, ALU.subtract).then_inc(f_z.sem, 1)
                        dve.wait_ge(f_ez.sem, at(f_ez, l))
                        nc.vector.reduce_sum(fsm[:, 0:1], fc[:, :], AX.X).then_inc(f_es.sem, 1)
                        dve.wait_ge(f_ln.sem, at(f_ln, l))
                        link(tsc(fc[:, :], fa[:, :], fsm[:, 1:2], None, ALU.subtract))
                        link(tt(fb[:, :], fc[:, :], rx[:, 1, :], ALU.add))
                    link(nc.vector.reduce_sum(fsm[:, 2:3], fb[:, :], AX.X))
                    link(tsc(fsm[:, 3:4], fsm[:, 2:3], 1.0 / D, None, ALU.mult))
                    tsc(fcen[:, :], fb[:, :], fsm[:, 3:4], None, ALU.subtract).then_inc(f_cen.sem, 1)
                    dve.wait_ge(f_rstd.sem, at(f_rstd, l))
                    tsc(fix[:, :], fcen[:, :], fsm[:, 6:7], ends[:, 0:1], ALU.mult, ALU.mult).then_inc(fix_ready.sem, 1)
                    if l < 3:
                        dve.wait_ge(fix_T.sem, at(fix_T, l))
                        link(nc.vector.memset(cR[:, P:P + 1], 0.0))
                        link(nc.vector.tensor_copy(ctile["a"][0:D, :], psX[0][0:D, 0:P]))
                        nc.vector.tensor_tensor_scan(cR[:, 0:P][:, ::-1], ctile["noend"][0:D, ::-1], ctile["a"][0:D, ::-1], 0.0,
                                                     ALU.mult, ALU.add).then_inc(init_ready.sem, 1)
                        dve.wait_ge(init_T.sem, at(init_T, l))
                        link(nc.vector.tensor_copy(init[:, :], psX[1][:, 0:D]))
                        for p in (0, 1):
                            landed(dve, rows_out, l, Half(HALVES // 2 - 1, p))
                        for f in range(D):
                            ins = nc.vector.tensor_tensor_scan(feats[:, ::-1, f], notlast[:, ::-1], feats[:, ::-1, f], init[:, f:f + 1],
                                                               ALU.mult, ALU.add)
                        link(ins)
                    chain["dve"] = n[0]


_INS = ["x", "src", "dst", "edge_attr_64", "L0_gnn_Wq", "L0_gnn_bq", "L0_gnn_Wk", "L0_gnn_bk", "L0_gnn_Wv", "L0_gnn_bv",
        "L0_gnn_We", "L0_gnn_Ws", "L0_gnn_bs", "L0_gnn_ln_gamma", "L0_gnn_ln_beta", "L1_gnn_Wq", "L1_gnn_Wk", "L1_gnn_Wv",
        "L1_gnn_Wo"]


def kernel(**inputs):
    import numpy as np
    import concourse.bacc as bacc
    from concourse.bass_utils import run_bass_kernel_spmd

    nc = bacc.Bacc("TRN2", target_bir_lowering=False, num_devices=1)
    arrays, args = {}, []
    for name in _INS:
        a = np.ascontiguousarray(inputs[name])
        arrays[f"in_{name}"] = a
        args.append(nc.dram_tensor(f"in_{name}", a.shape, mybir.dt.from_np(a.dtype), kind="ExternalInput").ap())
    out = nc.dram_tensor("out_0", inputs["x"].shape, F32, kind="ExternalOutput").ap()
    gnn_kernel(nc, *args, out)
    return run_bass_kernel_spmd(nc, [arrays], core_ids=[0]).results[0]["out_0"]
```

```python
from contextlib import ExitStack

import concourse.bass as bass
from concourse import mybir

F32 = mybir.dt.float32
BF16 = mybir.dt.bfloat16
I32 = mybir.dt.int32
ALU = mybir.AluOpType
ACT = mybir.ActivationFunctionType
AX = mybir.AxisListType

P = 128
D = 64
C = 4
MAPC = 14
NODEC = 8
GROUP = 4
SPLIT = 112
NEVER = -1.0e30
SKIP = 1 << 20
HEADW = 16
LAYERS = (0, 1, 2, 3)


class Half:

    def __init__(self, i, par):
        self.i, self.par = i, par
        self.k = 2 * i + par

    def plus(self, off):
        n = self.par + off
        return Half(self.i + n // 2, n % 2)

    def exists(self, halves):
        return not isinstance(self.k, int) or 0 <= self.k < halves

    def cols(self):
        return bass.ds(self.k * C, C)


class Signal:

    def __init__(self, sem, halves, step=1, layers=LAYERS):
        self.sem, self.halves, self.step, self.layers = sem, halves, step, layers

    def at(self, layer, k, n=None):
        before = self.halves * sum(x < layer for x in self.layers)
        return k * self.step + (before * self.step + (self.step if n is None else n))


class Landing:

    def __init__(self, sems, halves, step=16, layers=LAYERS):
        self.sem, self.halves, self.step, self.layers = sems, halves, step, layers

    def at(self, layer, i):
        before = self.halves // 2 * sum(x < layer for x in self.layers)
        return i * self.step + (before + 1) * self.step


def wait(eng, sem, value):
    if not isinstance(value, int) or value > 0:
        eng.wait_ge(sem, value)


def after(eng, signal, layer, h):
    wait(eng, signal.sem, signal.at(layer, h.k))


def landed(eng, landing, layer, h):
    wait(eng, landing.sem[h.par], landing.at(layer, h.i))


def run(eng, halves, step, lo, hi):
    start, stop = 3, (halves - 3) // 2
    for s in range(lo, 2 * start):
        step(Half(s // 2, s % 2))
    with eng.Fori(start, stop) as i:
        step(Half(i, 0))
        step(Half(i, 1))
    for s in range(2 * stop, hi + 1):
        step(Half(s // 2, s % 2))


def stage(fn, h, off, halves):
    h = h.plus(off)
    if h.exists(halves):
        fn(h)


def gnn_kernel(nc, x, src, dst, edge_attr, Wq, bq, Wk, bk, Wv, bv, We, Ws, bs, gamma, beta, Wq1, Wk1, Wv1, Wo1, out):
    N, E = x.shape[0], src.shape[0]
    COLS = -(-E // (P * 2 * C)) * 2 * C
    HALVES = COLS // C
    EP = P * COLS
    LASTC = E - (P - 1) * COLS
    FULL = LASTC // C
    MAPH = COLS // MAPC
    BLOCK = P * NODEC
    BLOCKS = -(-N // BLOCK)
    TAILP = (N - (BLOCKS - 1) * BLOCK) // NODEC
    RUN = -(-N // P)
    while N % RUN:
        RUN += 1
    NH = D // HEADW
    R = D + NH
    assert LASTC % C == 0 and LASTC > 0 and COLS % MAPC == 0 and MAPH % 2 == 0 and HALVES % 2 == 0
    assert (BLOCKS - 1) * BLOCK + TAILP * NODEC == N and E % 16 == 0

    rows = [x] + [nc.dram_tensor(f"rows{l}", (N + EP, D), F32, kind="Internal").ap() for l in (1, 2, 3)]
    acc_d = nc.dram_tensor("acc_rows", (EP, D), F32, kind="Internal").ap()
    skip_d = nc.dram_tensor("skip_rows", (EP, D), F32, kind="Internal").ap()
    x0_d = nc.dram_tensor("x_at_dst", (EP, D), F32, kind="Internal").ap()
    etail_d = nc.dram_tensor("edge_tail", ((P - SPLIT) * COLS, D), F32, kind="Internal").ap()
    dpad = nc.dram_tensor("dst_padded", (EP + 2,), I32, kind="Internal").ap()
    where_d = nc.dram_tensor("row_of_node", (N, 1), I32, kind="Internal").ap()

    def by_edge(t):
        return t.rearrange("(p j) d -> p j d", p=P)

    with ExitStack() as ctx:
        def sb(name, shape, dt=F32):
            return ctx.enter_context(nc.sbuf_tensor(name, shape, dt))

        def sem(name):
            return ctx.enter_context(nc.semaphore(name))

        def signal(name, layers=LAYERS, step=1):
            return Signal(sem(name), HALVES, step, layers)

        def landing(name, layers=LAYERS, step=16):
            return Landing([sem(name + "_a"), sem(name + "_b")], HALVES, step, layers)

        def event(name, layers=LAYERS, step=1):
            return Signal(sem(name), 1, step, layers)

        feats = sb("feats", [P, COLS, D])
        src_i = sb("src_i", [P, COLS], I32)
        row_i = sb("row_i", [P, COLS], I32)
        cont = sb("cont", [P, COLS])
        notlast = sb("notlast", [P, COLS])
        pen = sb("pen", [P, COLS])
        lead = sb("lead", [P, COLS])
        leadend = sb("leadend", [P, COLS])
        ownlast = sb("ownlast", [P, COLS])
        out_i = sb("out_i", [P, COLS], I32)
        M = sb("M", [P, NH, COLS + 1])
        S = sb("S", [P, NH, COLS + 1])
        ident = sb("ident", [P, P])
        eps = sb("eps", [P, 1])
        ones3 = sb("ones3", [3, P], BF16)
        wkv = sb("wkv", [P, 3, 2 * D])
        wqs = sb("wqs", [P, 3, 2, 2 * D])
        wkv1 = sb("wkv1", [P, 2, 2 * D])
        wq1 = sb("wq1", [P, 2, D])
        wo1 = sb("wo1", [P, 2, D])
        gam = sb("gam", [P, 2])
        bet = sb("bet", [P, 2])
        bias3 = sb("bias3", [3, 3, 2, C, 2 * D], BF16)
        lead_i = sb("lead_i", [P, 3], I32)
        ends = sb("ends", [P, 4])
        fix = sb("fix", [P, D])
        dst_i = sb("dst_i", [P, COLS], I32)
        end_i = sb("end_i", [P, COLS], I32)
        pos_i = sb("pos_i", [P, COLS], I32)
        ctile = {s: sb("c_" + s, [R, P]) for s in ("m", "a", "mF", "f", "wpen", "cpen", "noend", "d1", "d2", "e1", "e2", "t")}
        idxr = sb("idxr", [P, 2, 2, C], I32)
        T = sb("T", [P, 2, C, 2, D])
        T3 = T[:].rearrange("p r c t d -> p r (c t) d")
        xs = sb("xs", [P, 2, C, D])
        fT = sb("fT", [P, 2, C * P])
        xT = sb("xT", [P, 2, 2 * P])
        qs = sb("qs", [P, 2, C, 2 * D])
        alpha = sb("alpha", [P, 2, NH * C])
        dif = sb("dif", [P, 2, 2, NH * C])
        ex = sb("ex", [P, 2, 2, NH * C])
        acc = sb("acc", [P, 2 * C, D])
        cen = sb("cen", [P, 2, C, D])
        var = sb("var", [P, 2, C])
        rstd = sb("rstd", [P, 2, C])
        x0 = sb("x0", [P, 2, C, D])
        yout = sb("yout", [P, 2, C, D])
        oidx = sb("oidx", [P, 2, C], I32)
        leadx = sb("leadx", [P, C, D])
        prod = sb("prod", [P, C, D])
        alphac = sb("alphac", [P, NH * C])
        dif0 = sb("dif0", [P, NH * C])
        pv = sb("pv", [P, C, D])
        carry = sb("carry", [P, D])
        stot = sb("stot", [P, NH * C])
        sinv = sb("sinv", [P, NH * C])
        t1 = sb("t1", [P, C, D])
        t2 = sb("t2", [P, C, D])
        t3 = sb("t3", [P, C, D])
        ez = sb("ez", [P, C, D])
        junk = sb("junk", [P, C, D])
        agT = sb("agT", [P, 2 * P])
        csum = sb("csum", [P, 2, C])
        mean = sb("mean", [P, C])
        hmax = sb("hmax", [P, C])
        esum = sb("esum", [P, C])
        lns = sb("lns", [P, C])
        lnv = sb("lnv", [P, C])
        rmask = sb("rmask", [P, C])

        psT = [ctx.enter_context(nc.psum_tensor(f"psT{i}", [P, 512], F32)) for i in (0, 1)]
        psX = [ctx.enter_context(nc.psum_tensor(f"psX{i}", [P, 512], F32)) for i in (0, 1)]
        psKV = [ctx.enter_context(nc.psum_tensor(f"psKV{i}", [P, 512], F32)) for i in (0, 1)]
        psQ = [ctx.enter_context(nc.psum_tensor(f"psQ{i}", [P, 512], F32)) for i in (0, 1)]

        with ExitStack() as tmp:
            def ts(name, shape, dt=F32):
                return tmp.enter_context(nc.sbuf_tensor(name, shape, dt))

            cur = ts("cur", [P, COLS], I32)
            nxt = ts("nxt", [P, COLS], I32)
            prv = ts("prv", [P, COLS], I32)
            padi = ts("padi", [1, EP - E + 2], I32)
            nodes = ts("nodes", [P, RUN], I32)
            last = ts("last", [P, COLS])
            zeros = ts("zeros", [P, COLS])
            f1 = ts("f1", [P, COLS])
            f2 = ts("f2", [P, COLS])
            brow = ts("brow", [1, 3, 4 * D])
            bsplit = ts("bsplit", [1, 3, 3, 4 * D], BF16)
            bres = ts("bres", [1, 3, 4 * D])
            lead_f = ts("lead_f", [P, 3])
            flagrows = ts("flagrows", [P, 3, R])
            flags_made, flags_T = sem("flags_made"), sem("flags_T")
            loaded, zeroed, padded, shifted = sem("loaded"), sem("zeroed"), sem("padded"), sem("shifted")
            split_ready, bias_in, consts, table_in = sem("split_ready"), sem("bias_in"), sem("consts"), sem("table_in")
            bias_mm, setup_n = sem("bias_mm"), sem("setup_n")

            w3 = "l a b -> a l b"
            jobs = [(wkv[0:D, :, 0:D], Wk.rearrange(w3)), (wkv[0:D, :, D:2 * D], Wv.rearrange(w3)),
                    (wkv[D:P, :, 0:D], We.rearrange(w3)), (wkv[D:P, :, D:2 * D], We.rearrange(w3))]
            for b in (0, D):
                j = b // D
                jobs += [(wqs[b:b + D, :, j, 0:D], Wq.rearrange(w3)), (wqs[b:b + D, :, j, D:2 * D], Ws.rearrange(w3)),
                         (wkv1[b:b + D, j, 0:D], Wk1), (wkv1[b:b + D, j, D:2 * D], Wv1),
                         (wq1[b:b + D, j, :], Wq1), (wo1[b:b + D, j, :], Wo1)]
                for l in (0, 1):
                    jobs += [(gam[b:b + D, l:l + 1], gamma[l:l + 1, :].rearrange("l d -> d l")),
                             (bet[b:b + D, l:l + 1], beta[l:l + 1, :].rearrange("l d -> d l"))]
            for j, bias in enumerate((bk, bv, bq, bs)):
                jobs += [(brow[:, :, j * D:(j + 1) * D], bias.rearrange("(a l) d -> a l d", a=1))]
            jobs += [(src_i[0:SPLIT, :], src[0:SPLIT * COLS].rearrange("(p j) -> p j", j=COLS)),
                     (src_i[SPLIT:P - 1, :], src[SPLIT * COLS:(P - 1) * COLS].rearrange("(p j) -> p j", j=COLS)),
                     (src_i[P - 1:P, 0:LASTC], src[(P - 1) * COLS:E].rearrange("(p j) -> p j", p=1))]
            with nc.Block() as block:
                @block.sync
                def _(sp):
                    sp.wait_ge(zeroed, 1)
                    sp.dma_start(dpad[1:E + 1].rearrange("(a n) -> a n", a=16), dst.rearrange("(a n) -> a n", a=16)).then_inc(padded, 16)
                    sp.dma_start(dpad[0:1].rearrange("(a n) -> a n", a=1), padi[:, 0:1]).then_inc(padded, 16)
                    sp.dma_start(dpad[E + 1:EP + 1].rearrange("(a n) -> a n", a=1), padi[:, 1:EP - E + 1]).then_inc(padded, 16)
                    sp.dma_start(dpad[EP + 1:EP + 2].rearrange("(a n) -> a n", a=1), padi[:, 0:1]).then_inc(padded, 16)
                    sp.wait_ge(padded, 64)
                    for off, tile in ((1, cur), (2, nxt), (0, prv)):
                        sp.dma_start(tile[:, :], dpad[off:off + EP].rearrange("(p j) -> p j", p=P)).then_inc(shifted, 16)
                    sp.dma_start(etail_d[0:E - SPLIT * COLS, :].rearrange("(a n) d -> a (n d)", a=16),
                                 edge_attr[SPLIT * COLS:E, :].rearrange("(a n) d -> a (n d)", a=16)).then_inc(padded, 16)
                    sp.dma_start(etail_d[E - SPLIT * COLS:, :].rearrange("r d -> (r d)").rearrange("(p n) -> p n", p=P),
                                 zeros[:, 0:(EP - E) * D // P]).then_inc(padded, 16)
                    sp.wait_ge(split_ready, 1)
                    for part in range(3):
                        for c in range(C):
                            sp.dma_start(bias3[part:part + 1, :, :, c, :],
                                         bsplit[0:1, part, :, :].rearrange("o l (t d) -> o l t d", t=2)).then_inc(bias_in, 16)
                    sp.wait_ge(padded, 96)
                    sp.wait_ge(bias_in, 16 * 3 * C)

                @block.scalar
                def _(act):
                    act.wait_ge(zeroed, 1)
                    for tile, source in jobs:
                        act.dma_start(tile, source).then_inc(loaded, 16)

                @block.gpsimd
                def _(pool):
                    nc.gpsimd.memset(ident[:, :], 0.0).then_inc(consts, 1)
                    pool.wait_ge(consts, 1)
                    nc.gpsimd.affine_select(out=ident[:, :], in_=ident[:, :], compare_op=ALU.not_equal, fill=1.0, base=0,
                                            pattern=[[-1, P]], channel_multiplier=1).then_inc(consts, 1)
                    nc.gpsimd.iota(pos_i[:, :], pattern=[[1, COLS]], base=N, channel_multiplier=COLS).then_inc(consts, 1)
                    nc.gpsimd.iota(nodes[:, :], pattern=[[1, RUN]], base=0, channel_multiplier=RUN).then_inc(consts, 1)
                    pool.wait_ge(consts, 4)
                    pool.dma_start(where_d.rearrange("(p j) o -> p (j o)", j=RUN), nodes[0:N // RUN, :]).then_inc(table_in, 16)
                    pool.wait_ge(table_in, 16)

                @block.tensor
                def _(pe):
                    pe.wait_ge(loaded, 16 * len(jobs))
                    for l in (1, 2):
                        nc.tensor.matmul(psQ[l - 1][0:1, 0:2 * D], bet[0:D, l - 1:l], wkv[0:D, l, :], start=True, stop=True)
                        nc.tensor.matmul(psQ[l - 1][0:1, 2 * D:4 * D], bet[0:D, l - 1:l], wqs[0:D, l, 0, :],
                                         start=True, stop=True).then_inc(bias_mm, 1)
                    pe.wait_ge(flags_made, 1)
                    pe.wait_ge(consts, 4)
                    for j in range(3):
                        ins = nc.tensor.transpose(psT[0][0:R, j * P:(j + 1) * P], flagrows[:, j, :], ident[:, :])
                    ins.then_inc(flags_T, 1)

                @block.vector
                def _(dve):
                    done = [0]

                    def link(ins):
                        done[0] += 1
                        ins.then_inc(setup_n, 1)
                        dve.wait_ge(setup_n, done[0])

                    for tile, value in ((src_i, 0), (eps, 1e-5), (ones3, 1.0), (T, 0.0), (xs, 0.0), (acc, 0.0),
                                        (fix, 0.0), (zeros, 0.0), (qs, 0.0),
                                        (wqs, 0.0), (wkv1, 0.0), (wq1, 0.0), (wo1, 0.0)):
                        nc.vector.memset(tile[:], value)
                    nc.vector.memset(feats[:, 0:GROUP * NODEC, :], 0.0)
                    nc.vector.memset(M[:, :, 0:1], NEVER)
                    nc.vector.memset(S[:, :, 0:1], 0.0)
                    nc.vector.memset(padi[:, 0:1], N + 1)
                    nc.vector.memset(padi[:, 1:], N).then_inc(zeroed, 1)
                    dve.wait_ge(zeroed, 1)
                    dve.wait_ge(loaded, 16 * len(jobs))
                    dve.wait_ge(bias_mm, 2)
                    for l in (1, 2):
                        link(nc.vector.tensor_tensor(brow[:, l, :], brow[:, l, :], psQ[l - 1][0:1, 0:4 * D], ALU.add))
                        link(nc.vector.tensor_scalar(wkv[0:D, l, :], wkv[0:D, l, :], gam[0:D, l - 1:l], None, ALU.mult))
                        link(nc.vector.tensor_scalar(wqs[:, l, :, :], wqs[:, l, :, :], gam[:, l - 1:l], None, ALU.mult))
                    link(nc.vector.tensor_copy(bsplit[:, 0], brow[:]))
                    link(nc.vector.tensor_tensor(bres[:], brow[:], bsplit[:, 0], ALU.subtract))
                    link(nc.vector.tensor_copy(bsplit[:, 1], bres[:]))
                    link(nc.vector.tensor_tensor(bres[:], bres[:], bsplit[:, 1], ALU.subtract))
                    nc.vector.tensor_copy(bsplit[:, 2], bres[:]).then_inc(split_ready, 1)
                    dve.wait_ge(shifted, 48)
                    dve.wait_ge(consts, 4)
                    tt, tsc = nc.vector.tensor_tensor, nc.vector.tensor_scalar
                    link(nc.vector.tensor_copy(dst_i[:, :], cur[:, :]))
                    link(tt(last[:, :], cur[:, :], nxt[:, :], ALU.not_equal))
                    link(tt(cont[:, :], cur[:, :], prv[:, :], ALU.is_equal))
                    link(tsc(notlast[:, :], last[:, :], -1.0, 1.0, ALU.mult, ALU.add))
                    link(tsc(pen[:, :], cont[:, :], -NEVER, NEVER, ALU.mult, ALU.add))
                    link(nc.vector.tensor_tensor_scan(lead[:, :], cont[:, :], zeros[:, :], 1.0, ALU.mult, ALU.add))
                    link(tt(leadend[:, :], lead[:, :], last[:, :], ALU.mult))
                    link(tt(ownlast[:, :], last[:, :], leadend[:, :], ALU.subtract))

                    def masked(flag, value, tile):
                        link(tsc(f1[:, :], value, float(-SKIP), None, ALU.add))
                        link(tt(f1[:, :], f1[:, :], flag, ALU.mult))
                        link(tsc(tile[:, :], f1[:, :], float(SKIP), None, ALU.add))

                    masked(last[:, :], cur[:, :], end_i)
                    masked(ownlast[:, :], cur[:, :], out_i)
                    link(nc.vector.reduce_sum(ends[:, 0:1], leadend[:, :], AX.X))
                    link(tsc(ends[:, 1:2], ends[:, 0:1], -1.0, 1.0, ALU.mult, ALU.add))
                    link(nc.vector.tensor_copy(ends[:, 2:3], lead[:, COLS - 1:COLS]))
                    link(nc.vector.tensor_copy(ends[:, 3:4], cont[:, 0:1]))
                    for j, value in ((0, pos_i), (2, cur)):
                        link(tt(f2[:, :], leadend[:, :], value[:, :], ALU.mult))
                        link(nc.vector.reduce_sum(lead_f[:, j:j + 1], f2[:, :], AX.X))
                    link(tsc(lead_f[:, 1:2], lead_f[:, 0:1], 1.0, None, ALU.mult))
                    link(tsc(lead_f[:, 0:1], lead_f[:, 0:1], float(-N), None, ALU.add))
                    link(tsc(lead_f[:, :], lead_f[:, :], float(-SKIP), ends[:, 0:1], ALU.add, ALU.mult))
                    link(tsc(lead_i[:, :], lead_f[:, :], float(SKIP), None, ALU.add))

                    link(tsc(flagrows[:, 0, :], ends[:, 2:3].broadcast_to([P, R]), -NEVER, NEVER, ALU.mult, ALU.add))
                    link(tsc(flagrows[:, 1, :], ends[:, 3:4].broadcast_to([P, R]), -NEVER, NEVER, ALU.mult, ALU.add))
                    nc.vector.tensor_copy(flagrows[:, 2, :], ends[:, 1:2].broadcast_to([P, R])).then_inc(flags_made, 1)
                    dve.wait_ge(flags_T, 1)
                    for j, k in enumerate(("wpen", "cpen", "noend")):
                        link(nc.vector.tensor_copy(ctile[k][:, :], psT[0][0:R, j * P:(j + 1) * P]))
        with ExitStack() as tmp:
            def ts(name, shape, dt=F32):
                return tmp.enter_context(nc.sbuf_tensor(name, shape, dt))

            mapidx = ts("mapidx", [P, 2, MAPC], I32)
            mapval = ts("mapval", [P, 2, MAPC], I32)
            def carve(first, n):
                part = feats[:, first * NODEC:(first + GROUP * n) * NODEC, :].rearrange("p (r c) d -> p r c d", r=GROUP)
                return part, first + GROUP * n
            nx, at_ = carve(0, 1)
            na, at_ = carve(at_, 1)
            nb, at_ = carve(at_, 1)
            ncen, at_ = carve(at_, 1)
            nsq, at_ = carve(at_, 1)
            nT, at_ = carve(at_, 1)
            nT = nT.rearrange("p r c d -> p r (c d)")
            nval, at_ = carve(at_, 4)
            nval = nval.rearrange("p r (t c) d -> p r t c d", t=4)
            nsmall = ts("nsmall", [P, GROUP, 2, NODEC])
            nvar = ts("nvar", [P, GROUP, NODEC])
            nlnv = ts("nlnv", [P, GROUP, NODEC])
            nrstd = ts("nrstd", [P, GROUP, NODEC])
            GROUPS = BLOCKS // GROUP
            assert BLOCKS % GROUP == 1
            psA, psB = psT + psX, psQ + psKV

            class NodeSignal:

                def __init__(self, name, steps):
                    self.sem, self.steps = sem(name), steps

                def at(self, group, t, blk):
                    if isinstance(group, int) and group == GROUPS:
                        return GROUPS * GROUP * self.steps + t + 1
                    return group * (GROUP * self.steps) + (GROUP * t + blk + 1)

                def wait(self, eng, group, t, blk):
                    wait(eng, self.sem, self.at(group, t, blk))

            n_tr, n_ev, n_mm, n_relu = (NodeSignal(s, 3) for s in ("n_tr", "n_ev", "n_mm", "n_relu"))
            n_val = NodeSignal("n_val", 4)
            n_cen, n_sq, n_var, n_lv, n_rstd = (NodeSignal(s, 4) for s in ("n_cen", "n_sq", "n_var", "n_lv", "n_rstd"))
            n_z, n_ez, n_es, n_ln = (NodeSignal(s, 1) for s in ("n_z", "n_ez", "n_es", "n_ln"))
            n_link = sem("n_link")
            nld = [sem(f"nld_{b}") for b in range(GROUP)]
            nst = [[sem(f"nst{t}_{b}") for b in range(GROUP)] for t in range(4)]
            map_in = [sem("map_in_a"), sem("map_in_b")]
            map_done = [sem("map_done_a"), sem("map_done_b")]
            map_kept = [sem("map_kept_a"), sem("map_kept_b")]
            pool_step = sem("pool_step")

            def block_rows(t, group, blk):
                if isinstance(group, int) and group == GROUPS:
                    return t[GROUPS * GROUP * BLOCK:N, :].rearrange("(p c) d -> p c d", c=NODEC)
                v = t[0:GROUPS * GROUP * BLOCK, :].rearrange("(b p c) d -> b p (c d)", p=P, c=NODEC)
                return v[bass.ds(GROUP * group + blk, 1), :, :].rearrange("b p (c d) -> (b p) c d", c=NODEC)

            def parts(group):
                return TAILP if isinstance(group, int) and group == GROUPS else P

            def blocks(group):
                return range(1 if isinstance(group, int) and group == GROUPS else GROUP)

            def early(group):
                return blocks(group)[:GROUP // 2]

            def late(group):
                return blocks(group)[GROUP // 2:]

            def late_before(i, t):
                if t > 0:
                    return i, t - 1, late(i)
                if isinstance(i, int) and i == 0:
                    return 0, 3, ()
                return i + (-1), 3, late(GROUPS - 1)

            def over_groups(eng, body):
                body(0)
                body(1)
                with eng.Fori(2, GROUPS - 1) as i:
                    body(i)
                body(GROUPS - 1)
                body(GROUPS)

            with nc.Block() as block:
                @block.sync
                def _(sp):
                    W1 = MAPH // 2
                    for phase in (0, 1):
                        def ring(i, par):
                            cols = bass.ds((2 * i + par) * MAPC, MAPC)
                            wait(sp, map_done[par], (i + phase * W1) * (16 * MAPC))
                            if phase == 0:
                                sp.dma_start(mapidx[:, par, :], end_i[:, cols]).then_inc(map_in[par], 16)
                                sp.dma_start(mapval[:, par, :], pos_i[:, cols]).then_inc(map_in[par], 16)
                                return
                            if not (isinstance(i, int) and i == 0):
                                sp.dma_start(row_i[:, bass.ds((2 * i + par - 2) * MAPC, MAPC)],
                                             mapval[:, par, :]).then_inc(map_kept[par], 16)
                                wait(sp, map_kept[par], i * 16)
                            sp.dma_start(mapidx[:, par, :], src_i[:, cols]).then_inc(map_in[par], 16)
                        for par in (0, 1):
                            ring(0, par)
                        with sp.Fori(1, W1) as i:
                            ring(i, 0)
                            ring(i, 1)
                    for par in (0, 1):
                        sp.wait_ge(map_done[par], MAPH * 16 * MAPC)
                        j = (MAPH - 2 + par) * MAPC
                        sp.dma_start(row_i[:, j:j + MAPC], mapval[:, par, :]).then_inc(map_kept[par], 16)
                        sp.wait_ge(map_kept[par], W1 * 16)

                @block.gpsimd
                def _(pool):
                    last_node = pool.to_reg(N - 1)
                    W1 = MAPH // 2
                    with pool.Fori(0, W1) as i:
                        for par in (0, 1):
                            pool.wait_ge(map_in[par], i * 32 + 32)
                            pool.sem_inc(pool_step, 1)
                            for j in range(MAPC):
                                nc.gpsimd.indirect_dma_start(
                                    where_d, bass.IndirectOffsetOnAxis(mapidx[:, par, j:j + 1], 0), mapval[:, par, j:j + 1], None,
                                    bounds_check=last_node, oob_is_err=False).then_inc(map_done[par], 16)
                    for par in (0, 1):
                        pool.wait_ge(map_done[par], W1 * 16 * MAPC)
                    with pool.Fori(0, W1) as i:
                        for par in (0, 1):
                            pool.wait_ge(map_in[par], i * 16 + (W1 * 32 + 16))
                            pool.sem_inc(pool_step, 1)
                            for j in range(MAPC):
                                nc.gpsimd.indirect_dma_start(
                                    mapval[:, par, j:j + 1], None, where_d, bass.IndirectOffsetOnAxis(mapidx[:, par, j:j + 1], 0),
                                    bounds_check=last_node, oob_is_err=False).then_inc(map_done[par], 16)

                @block.tensor
                def _(pe):
                    def turn(i, t, b):
                        if t == 0:
                            pe.wait_ge(nld[b], i * 16 + 16)
                        else:
                            n_val.wait(pe, i, t - 1, b)
                        source = nx[:, b] if t == 0 else nval[:, b, t - 1]
                        for g in range(NODEC // 2):
                            ins = nc.tensor.transpose(psA[b][:, g * P:(g + 1) * P],
                                                      source[:, 2 * g:2 * g + 2, :].rearrange("p c d -> p (c d)"), ident[:, :])
                        ins.then_inc(n_tr.sem, 1)

                    def skip_term(i, t, b):
                        n_ev.wait(pe, i, t, b)
                        for g in range(NODEC // C):
                            nc.tensor.matmul(psB[b][:, g * C * D:(g + 1) * C * D], ones3[:, :], bias3[:, t, 1, :, D:2 * D],
                                             start=(g == 0), stop=False)
                        for g in range(NODEC // 2):
                            ins = nc.tensor.matmul(psB[b][:, g * P:(g + 1) * P], nT[:, b, g * P:(g + 1) * P],
                                                   wqs[:, t, :, D:2 * D], start=False, stop=(g == NODEC // 2 - 1))
                        ins.then_inc(n_mm.sem, 1)

                    def body(i):
                        for t in range(3):
                            for part in (early(i), late(i)):
                                for b in part:
                                    turn(i, t, b)
                                for b in part:
                                    skip_term(i, t, b)
                    over_groups(pe, body)

                @block.scalar
                def _(act):
                    act.preload_act_table_set("natural_log_exp_and_others")

                    def load(i, b):
                        act.dma_start(nx[0:parts(i), b, :, :], block_rows(x, i, b)).then_inc(nld[b], 16)

                    def store(i, t, part):
                        for b in part:
                            n_val.wait(act, i, t, b)
                            act.dma_start(block_rows(out if t == 3 else rows[t + 1], i, b),
                                          nval[0:parts(i), b, t, :, :]).then_inc(nst[t][b], 16)

                    def turned(i, t, part):
                        for b in part:
                            n_tr.wait(act, i, t, b)
                            nc.scalar.copy(nT[:, b, :], psA[b][:, :]).then_inc(n_ev.sem, 1)

                    def relu(i, t, part):
                        for b in part:
                            n_mm.wait(act, i, t, b)
                            nc.scalar.activation(na[:, b], psB[b][:, :].rearrange("p (c d) -> p c d", d=D), ACT.Relu).then_inc(n_relu.sem, 1)

                    def softmax(i, part):
                        for b in part:
                            n_z.wait(act, i, 0, b)
                            nc.scalar.activation(nb[:, b], na[:, b], ACT.Exp).then_inc(n_ez.sem, 1)
                        for b in part:
                            n_es.wait(act, i, 0, b)
                            nc.scalar.activation(nsmall[:, b, 0, :], nsmall[:, b, 1, :], ACT.Ln).then_inc(n_ln.sem, 1)

                    def squares(i, t, part):
                        for b in part:
                            n_cen.wait(act, i, t, b)
                            if t == 2 and not (isinstance(i, int) and (i == GROUPS or i == GROUPS - 1 and b > 0)):
                                load(i + 1, b)
                            nc.scalar.activation(nsq[:, b], ncen[:, b], ACT.Square).then_inc(n_sq.sem, 1)

                    def scales(i, t, part):
                        for b in part:
                            n_var.wait(act, i, t, b)
                            nc.scalar.activation(nlnv[:, b, :], nvar[:, b, :], ACT.Ln, bias=eps[:, 0:1], scale=1.0 / D).then_inc(n_lv.sem, 1)
                        for b in part:
                            n_lv.wait(act, i, t, b)
                            nc.scalar.activation(nrstd[:, b, :], nlnv[:, b, :], ACT.Exp, scale=-0.5).then_inc(n_rstd.sem, 1)

                    def body(i):
                        for t in range(4):
                            A, B, before = early(i), late(i), late_before(i, t)
                            if t < 3:
                                turned(i, t, A)
                                relu(i, t, A)
                            if t > 0:
                                store(i, t - 1, A)
                            elif not isinstance(i, int) or i > 0:
                                store(i + (-1), 3, early(GROUPS - 1))
                            squares(*before)
                            if t == 2:
                                softmax(i, A)
                            squares(i, t, A)
                            scales(*before)
                            if t < 3:
                                turned(i, t, B)
                            scales(i, t, A)
                            if t < 3:
                                relu(i, t, B)
                            store(*before)
                            if t == 2:
                                softmax(i, B)
                    for b in range(GROUP):
                        load(0, b)
                    over_groups(act, body)
                    store(GROUPS, 3, early(GROUPS))
                    for t in range(4):
                        for b in range(GROUP):
                            act.wait_ge(nst[t][b], 16 * (GROUPS + (b == 0)))

                @block.vector
                def _(dve):
                    LINKS = 11
                    tt, tsc = nc.vector.tensor_tensor, nc.vector.tensor_scalar

                    def body(i):
                        n = [0]
                        first = i * (GROUP * LINKS)

                        def count(ins):
                            n[0] += 1
                            ins.then_inc(n_link, 1)
                            return n[0]

                        def need(step):
                            dve.wait_ge(n_link, first + step)

                        def wide(small):
                            return small.unsqueeze(2).broadcast_to([P, NODEC, D])

                        def log_softmax(part):
                            maxima, logs, sums = {}, {}, {}
                            for b in part:
                                n_relu.wait(dve, i, 2, b)
                                maxima[b] = count(nc.vector.reduce_max(nsmall[:, b, 0, :], na[:, b], AX.X))
                            for b in part:
                                need(maxima[b])
                                tt(na[:, b], na[:, b], wide(nsmall[:, b, 0, :]), ALU.subtract).then_inc(n_z.sem, 1)
                            for b in part:
                                n_ez.wait(dve, i, 0, b)
                                nc.vector.reduce_sum(nsmall[:, b, 1, :], nb[:, b], AX.X).then_inc(n_es.sem, 1)
                            for b in part:
                                n_ln.wait(dve, i, 0, b)
                                logs[b] = count(tt(nb[:, b], na[:, b], wide(nsmall[:, b, 0, :]), ALU.subtract))
                            for b in part:
                                need(logs[b])
                                sums[b] = count(tt(na[:, b], nb[:, b], nx[:, b], ALU.add))
                            return sums

                        def centre(t, part):
                            ready = log_softmax(part) if t == 2 else None
                            h = {b: na[:, b] if t < 3 else nval[:, b, 2] for b in part}
                            sums, means = {}, {}
                            for b in part:
                                if t < 2:
                                    n_relu.wait(dve, i, t, b)
                                elif t == 2:
                                    need(ready[b])
                                else:
                                    n_val.wait(dve, i, 2, b)
                                sums[b] = count(nc.vector.reduce_sum(nsmall[:, b, 0, :], h[b], AX.X))
                            for b in part:
                                need(sums[b])
                                means[b] = count(tsc(nsmall[:, b, 1, :], nsmall[:, b, 0, :], 1.0 / D, None, ALU.mult))
                            for b in part:
                                need(means[b])
                                tt(ncen[:, b], h[b], wide(nsmall[:, b, 1, :]), ALU.subtract).then_inc(n_cen.sem, 1)

                        def normalise(group, t, part):
                            for b in part:
                                n_sq.wait(dve, group, t, b)
                                nc.vector.reduce_sum(nvar[:, b, :], nsq[:, b], AX.X).then_inc(n_var.sem, 1)
                            for b in part:
                                n_rstd.wait(dve, group, t, b)
                                wait(dve, nst[t][b], group * 16)
                                tt(nval[:, b, t], ncen[:, b], wide(nrstd[:, b, :]), ALU.mult).then_inc(n_val.sem, 1)

                        for t in range(4):
                            centre(t, early(i))
                            normalise(*late_before(i, t))
                            normalise(i, t, early(i))
                            centre(t, late(i))
                        assert n[0] == len(blocks(i)) * LINKS
                    over_groups(dve, body)
        chain = {}
        lead_x, xs_ready = signal("lead_x", (1, 2, 3)), signal("xs_ready", (1, 2, 3))
        gathered, gathered_x = landing("gathered", step=16 * C), landing("gathered_x", (0,), 16 * C)
        edges_in, x0_in = landing("edges_in", (0, 1, 2), 32), landing("x0_in", (2,))
        acc_out, skip_out, rows_out = landing("acc_out"), landing("skip_out", (0, 1, 2)), landing("rows_out", (0, 1, 2))
        x0_out, out_done = landing("x0_out", (0,)), landing("out_done", (3,), 16 * C)
        idx_ready, transposed, fT_ready = signal("idx_ready"), signal("transposed"), signal("fT_ready")
        xT_ready, kv_ready, q_ready, qs_ready = signal("xT_ready", (0, 1, 2)), signal("kv_ready"), signal("q_ready"), signal("qs_ready")
        prod_done, alpha_done, floor_done = signal("prod_done"), signal("alpha_done"), signal("floor_done", (3,))
        max_done, dif0_done, dif_ready, exp_ready = (signal(s) for s in ("max_done", "dif0_done", "dif_ready", "exp_ready"))
        sum_done, pv_done, seps_done, sinv_done = signal("sum_done"), signal("pv_done"), signal("seps_done"), signal("sinv_done")
        carried, acc_step = signal("carried", (3,), C), signal("acc_step", step=C)
        norm_done, added, relu_done = signal("norm_done"), signal("added"), signal("relu_done", (0, 1, 2))
        agT_made, agT_ready, wo_ready = signal("agT_made", (3,)), signal("agT_ready", (3,)), signal("wo_ready", (3,))
        hmax_done, z_ready, ez_ready, esum_ready = (signal(s, (2,)) for s in ("hmax_done", "z_ready", "ez_ready", "esum_ready"))
        ln_ready, lsm_done, res_done = (signal(s, (2,)) for s in ("ln_ready", "lsm_done", "res_done"))
        res_ready = signal("res_ready", (3,))
        fsum_done = signal("fsum_done", (2, 3))
        mean_done, cen_ready, rmask_done = (signal(s) for s in ("mean_done", "cen_ready", "rmask_done"))
        square_done, lnv_done, rstd_ready, value_ready = (signal(s) for s in ("square_done", "lnv_done", "rstd_ready", "value_ready"))
        oidx_ready = signal("oidx_ready", (3,))
        fix_preset, fix_ready, fix_in, fix_out = event("fix_preset"), event("fix_ready"), sem("fix_in"), event("fix_out", step=16)
        ends_ready, ends_T, tot_ready, tot_T = (event(s) for s in ("ends_ready", "ends_T", "tot_ready", "tot_T"))
        w_ready, w_exp, m_ready, m_exp = (event(s) for s in ("w_ready", "w_exp", "m_ready", "m_exp"))
        f_agg, f_aggT, f_aggTs, f_wo = (event(s, (3,)) for s in ("f_agg", "f_aggT", "f_aggTs", "f_wo"))
        f_z, f_ez, f_es, f_ln = (event(s, (2,)) for s in ("f_z", "f_ez", "f_es", "f_ln"))
        f_cen, f_sq, f_lv, f_rstd = (event(s) for s in ("f_cen", "f_sq", "f_lv", "f_rstd"))
        fix_T, init_ready, init_T = (event(s, (0, 1, 2)) for s in ("fix_T", "init_ready", "init_T"))
        c_link, s_link = sem("c_link"), sem("s_link")

        def at(e, l):
            return e.at(l, 0)

        big = sb("big", [P, NH, COLS])
        cG, cA, cR = sb("cG", [R, P + 1]), sb("cA", [R, P + 1]), sb("cR", [D, P + 1])
        rm, ra, rmF, rf, rt = (sb("r_" + s, [P, R]) for s in ("m", "a", "mF", "f", "t"))
        rx = sb("rx", [P, 2, D])
        fa, fb, fc, fcen = (sb("f_" + s, [P, D]) for s in ("a", "b", "c", "cen"))
        faggT = sb("f_T", [D, P])
        fsm = sb("fsm", [P, 8])
        init = sb("init", [P, D])

        for l in LAYERS:
            H = NH if l == 3 else 1
            F = D // H
            RL = D + H
            SCALE = float(F) ** -0.5
            lag = 3
            G = 2 * D if l < 3 else D

            def heads(tile, n=C):
                return tile[:, 0:H * n].rearrange("p (h c) -> p h c", h=H)

            def over_features(small):
                return small.rearrange("p h c -> p c h").unsqueeze(3).broadcast_to([P, C, H, F])

            def split(t):
                return t.rearrange("p c (h f) -> p c h f", h=H)

            def wide(small):
                return small.unsqueeze(2).broadcast_to([P, C, D])

            def link_from(eng, semaphore, start):
                n = [start]

                def link(ins):
                    n[0] += 1
                    ins.then_inc(semaphore, 1)
                    eng.wait_ge(semaphore, n[0])
                return link, n

            with nc.Block() as block:
                @block.sync
                def _(sp):
                    def load(h):
                        after(sp, transposed, l, h.plus(-2))
                        for lo, hi, t in ((0, SPLIT, edge_attr[0:SPLIT * COLS, :]), (SPLIT, P, etail_d)):
                            e = t.rearrange("(p j) d -> p j d", j=COLS)
                            sp.dma_start(T[lo:hi, h.par, :, 1, :], e[:, h.cols(), :]).then_inc(edges_in.sem[h.par], 16)

                    def load_x0(h):
                        after(sp, res_done, l, h.plus(-2))
                        sp.dma_start(x0[:, h.par, :, :], by_edge(x0_d)[:, h.cols(), :]).then_inc(x0_in.sem[h.par], 16)

                    def keep(h):
                        landed(sp, gathered_x, l, h)
                        sp.dma_start(by_edge(x0_d)[:, h.cols(), :], xs[:, h.par, :, :]).then_inc(x0_out.sem[h.par], 16)

                    def store_skip(h):
                        after(sp, qs_ready, l, h)
                        sp.dma_start(by_edge(skip_d)[:, h.cols(), :], qs[:, h.par, :, D:2 * D]).then_inc(skip_out.sem[h.par], 16)

                    def store(h):
                        after(sp, acc_step, l, h)
                        sp.dma_start(by_edge(acc_d)[:, h.cols(), :], acc[:, h.par * C:(h.par + 1) * C, :]).then_inc(acc_out.sem[h.par], 16)

                    def store_value(h):
                        after(sp, value_ready, l, h)
                        sp.dma_start(by_edge(rows[l + 1][N:N + EP, :])[:, h.cols(), :], feats[:, h.cols(), :]).then_inc(rows_out.sem[h.par], 16)

                    def step(h):
                        if l < 3:
                            stage(store_skip, h, -1, HALVES)
                            stage(load, h, 2, HALVES)
                        if l == 2:
                            stage(load_x0, h, 0, HALVES)
                        if l == 0:
                            stage(keep, h, 1, HALVES)
                        stage(store, h, -1, HALVES)
                        if l < 3:
                            stage(store_value, h, -lag, HALVES)
                    run(sp, HALVES, step, -2, HALVES + lag - 1)
                    for landing_ in (acc_out, skip_out, rows_out, x0_out):
                        if l in landing_.layers:
                            for p in (0, 1):
                                landed(sp, landing_, l, Half(HALVES // 2 - 1, p))

                @block.gpsimd
                def _(pool):
                    bound = pool.to_reg(N - 1 if l == 0 else N + EP - 1)
                    last_node = pool.to_reg(N - 1)
                    last_pos = pool.to_reg(EP - 1)
                    last_row = pool.to_reg(N + EP - 1)

                    def gather_rows(tile, table, index, bnd, semaphore):
                        nc.gpsimd.indirect_dma_start(tile, None, table, bass.IndirectOffsetOnAxis(index, 0),
                                                     bounds_check=bnd, oob_is_err=False).then_inc(semaphore, 16)

                    def scatter_rows(table, index, tile, bnd, semaphore):
                        nc.gpsimd.indirect_dma_start(table, bass.IndirectOffsetOnAxis(index, 0), tile, None,
                                                     bounds_check=bnd, oob_is_err=False).then_inc(semaphore, 16)

                    def gather(h):
                        after(pool, transposed, l, h.plus(-2))
                        after(pool, idx_ready, l, h)
                        if l == 0:
                            landed(pool, x0_out, l, h.plus(-2))
                        pool.sem_inc(pool_step, 1)
                        for c in range(C):
                            gather_rows(T[:, h.par, c, 0, :] if l < 3 else T3[:, h.par, c, :], rows[l], idxr[:, h.par, 0, c:c + 1], bound, gathered.sem[h.par])
                            if l == 0:
                                gather_rows(xs[:, h.par, c, :], rows[0], idxr[:, h.par, 1, c:c + 1], bound, gathered_x.sem[h.par])

                    def scatter(h):
                        after(pool, oidx_ready, l, h)
                        after(pool, value_ready, l, h)
                        pool.sem_inc(pool_step, 1)
                        for c in range(C):
                            scatter_rows(out, oidx[:, h.par, c:c + 1], yout[:, h.par, c, :], last_node, out_done.sem[h.par])

                    def lead_part(h):
                        after(pool, xs_ready, l, h.plus(-1))
                        nc.gpsimd.tensor_tensor(leadx[:, :, :], wide(lead[:, h.cols()]), fix[:, :].unsqueeze(1).broadcast_to([P, C, D]),
                                                ALU.mult).then_inc(lead_x.sem, 1)

                    def inputs(h):
                        after(pool, transposed, l, h.plus(-2))
                        after(pool, lead_x, l, h)
                        nc.gpsimd.tensor_tensor(xs[:, h.par, :, :], leadx[:, :, :], feats[:, h.cols(), :], ALU.add).then_inc(xs_ready.sem, 1)

                    def step(h):
                        stage(gather, h, 2, HALVES)
                        if l == 2:
                            stage(lead_part, h, 2, HALVES)
                        if l in (1, 2):
                            stage(inputs, h, 2, HALVES)
                        if l == 3:
                            stage(scatter, h, -lag, HALVES)
                    run(pool, HALVES, step, -2, HALVES + lag - 1)
                    for p in (0, 1):
                        for landing_ in (acc_out, skip_out, out_done, rows_out):
                            if l in landing_.layers:
                                landed(pool, landing_, l, Half(HALVES // 2 - 1, p))
                    pool.wait_ge(fix_preset.sem, at(fix_preset, l))
                    pool.sem_inc(pool_step, 1)
                    gather_rows(rf[:, 0:D], acc_d, lead_i[:, 0:1], last_pos, fix_in)
                    if l < 3:
                        gather_rows(rx[:, 0, :], skip_d, lead_i[:, 0:1], last_pos, fix_in)
                        gather_rows(rx[:, 1, :], x0_d, lead_i[:, 0:1], last_pos, fix_in)
                    pool.wait_ge(fix_ready.sem, at(fix_ready, l))
                    pool.sem_inc(pool_step, 1)
                    if l < 3:
                        scatter_rows(rows[l + 1], lead_i[:, 1:2], fix[:, :], last_row, fix_out.sem)
                    else:
                        scatter_rows(out, lead_i[:, 2:3], fix[:, :], last_node, fix_out.sem)
                    pool.wait_ge(fix_out.sem, at(fix_out, l))

                @block.tensor
                def _(pe):
                    def transposes(h):
                        p = h.par
                        landed(pe, gathered, l, h)
                        if l < 3:
                            landed(pe, edges_in, l, h)
                        if l == 0:
                            landed(pe, gathered_x, l, h)
                        else:
                            after(pe, xs_ready, l, h)
                        after(pe, fT_ready, l, h.plus(-2))
                        if l < 3:
                            after(pe, xT_ready, l, h.plus(-2))
                            for c in range(C):
                                nc.tensor.transpose(psT[p][:, c * P:(c + 1) * P], T[:, p, c, :, :].rearrange("p t d -> p (t d)"), ident[:, :])
                        else:
                            for g in range(2):
                                nc.tensor.transpose(psT[p][:, g * P:(g + 1) * P],
                                                    T3[:, p, 2 * g:2 * g + 2, :].rearrange("p c d -> p (c d)"), ident[:, :])
                        for g in range(2):
                            o = psX[p][:, g * P:(g + 1) * P] if l < 3 else psT[p][:, (2 + g) * P:(3 + g) * P]
                            ins = nc.tensor.transpose(o, xs[:, p, 2 * g:2 * g + 2, :].rearrange("p c d -> p (c d)"), ident[:, :])
                        ins.then_inc(transposed.sem, 1)

                    def products(h):
                        p = h.par
                        after(pe, prod_done, l, h.plus(-2))
                        after(pe, pv_done, l, h.plus(-2))
                        after(pe, fT_ready, l, h)
                        if l < 3:
                            nc.tensor.matmul(psKV[p][:, :], ones3[:, :], bias3[:, l, 0, :, :], start=True, stop=False)
                            for c in range(C):
                                ins = nc.tensor.matmul(psKV[p][:, c * P:(c + 1) * P], fT[:, p, c * P:(c + 1) * P], wkv[:, l, :],
                                                       start=False, stop=(c == C - 1))
                        else:
                            for g in range(2):
                                ins = nc.tensor.matmul(psKV[p][:, g * 2 * P:(g + 1) * 2 * P], fT[:, p, g * P:(g + 1) * P], wkv1[:, :, :],
                                                       start=True, stop=True)
                        ins.then_inc(kv_ready.sem, 1)
                        after(pe, qs_ready, l, h.plus(-2))
                        if l < 3:
                            after(pe, xT_ready, l, h)
                            nc.tensor.matmul(psQ[p][:, :], ones3[:, :], bias3[:, l, 1, :, :], start=True, stop=False)
                        for g in range(2):
                            w = xT[:, p, g * P:(g + 1) * P] if l < 3 else fT[:, p, (2 + g) * P:(3 + g) * P]
                            ins = nc.tensor.matmul(psQ[p][:, g * 2 * G:(g + 1) * 2 * G], w, wqs[:, l, :, :] if l < 3 else wq1[:, :, :],
                                                   start=(l == 3), stop=(l == 3 or g == 1))
                        ins.then_inc(q_ready.sem, 1)

                    def agg_turned(h):
                        after(pe, norm_done, l, h)
                        after(pe, agT_ready, l, h.plus(-1))
                        for g in range(2):
                            ins = nc.tensor.transpose(psX[0][:, g * P:(g + 1) * P],
                                                      t1[:, 2 * g:2 * g + 2, :].rearrange("p c d -> p (c d)"), ident[:, :])
                        ins.then_inc(agT_made.sem, 1)

                    def agg_product(h):
                        after(pe, agT_ready, l, h)
                        after(pe, added, l, h.plus(-1))
                        for g in range(2):
                            ins = nc.tensor.matmul(psX[1][:, g * P:(g + 1) * P], agT[:, g * P:(g + 1) * P], wo1[:, :, :],
                                                   start=True, stop=True)
                        ins.then_inc(wo_ready.sem, 1)

                    def step(h):
                        stage(products, h, 0, HALVES)
                        if l == 3:
                            stage(agg_turned, h, -2, HALVES)
                        stage(transposes, h, 1, HALVES)
                        if l == 3:
                            stage(agg_product, h, -2, HALVES)
                    run(pe, HALVES, step, -1, HALVES + 1)
                    pe.wait_ge(ends_ready.sem, at(ends_ready, l))
                    for j, t in enumerate((rm, ra, rmF, rf)):
                        ins = nc.tensor.transpose(psT[0][0:RL, j * P:(j + 1) * P], t[:, 0:RL], ident[:, :])
                    ins.then_inc(ends_T.sem, 1)
                    pe.wait_ge(tot_ready.sem, at(tot_ready, l))
                    nc.tensor.transpose(psT[1][:, 0:RL], ctile["t"][0:RL, :], ident[0:RL, 0:RL]).then_inc(tot_T.sem, 1)
                    if l == 3:
                        pe.wait_ge(f_agg.sem, at(f_agg, l))
                        nc.tensor.transpose(psX[0][0:D, 0:P], fa[:, :], ident[:, :]).then_inc(f_aggT.sem, 1)
                        pe.wait_ge(f_aggTs.sem, at(f_aggTs, l))
                        nc.tensor.matmul(psX[1][:, 0:D], faggT[0:D, :], wo1[0:D, 0, :], start=True, stop=True).then_inc(f_wo.sem, 1)
                    else:
                        pe.wait_ge(fix_ready.sem, at(fix_ready, l))
                        nc.tensor.transpose(psX[0][0:D, 0:P], fix[:, :], ident[:, :]).then_inc(fix_T.sem, 1)
                        pe.wait_ge(init_ready.sem, at(init_ready, l))
                        nc.tensor.transpose(psX[1][:, 0:D], cR[0:D, 1:P + 1], ident[0:D, 0:D]).then_inc(init_T.sem, 1)

                @block.scalar
                def _(act):
                    def evacuate(h):
                        p = h.par
                        after(act, transposed, l, h)
                        after(act, kv_ready, l, h.plus(-2))
                        after(act, q_ready, l, h.plus(-2))
                        nc.scalar.copy(fT[:, p, :], psT[p][:, :]).then_inc(fT_ready.sem, 1)
                        if l < 3:
                            nc.scalar.copy(xT[:, p, :], psX[p][:, 0:2 * P]).then_inc(xT_ready.sem, 1)

                    def indices(h):
                        p = h.par
                        landed(act, gathered, l, h.plus(-2))
                        if l == 0:
                            landed(act, gathered_x, l, h.plus(-2))
                            nc.scalar.copy(idxr[:, p, 1, :], dst_i[:, h.cols()])
                        nc.scalar.copy(idxr[:, p, 0, :], (src_i if l == 0 else row_i)[:, h.cols()]).then_inc(idx_ready.sem, 1)

                    def queries(h):
                        p = h.par
                        after(act, q_ready, l, h)
                        after(act, added if l < 3 else prod_done, l, h.plus(-2))
                        if l < 3:
                            landed(act, skip_out, l, h.plus(-2))
                        nc.scalar.copy(qs[:, p, :, 0:G], psQ[p][:, 0:C * G].rearrange("p (c d) -> p c d", c=C)).then_inc(qs_ready.sem, 1)

                    def relu(h):
                        after(act, added, l, h)
                        after(act, cen_ready, l, h.plus(-2))
                        for c in range(C):
                            ins = nc.scalar.activation(yout[:, h.par, c, :], t2[:, c, :], ACT.Relu, accum_out=csum[:, h.par, c:c + 1])
                        ins.then_inc(relu_done.sem, 1)

                    def residual(h):
                        after(act, xs_ready, l, h)
                        after(act, added, l, h.plus(-2))
                        nc.scalar.copy(x0[:, h.par, :, :], xs[:, h.par, :, :]).then_inc(res_ready.sem, 1)

                    def variance(h):
                        p = h.par
                        after(act, cen_ready, l, h)
                        after(act, value_ready, l, h.plus(-2))
                        for c in range(C):
                            ins = nc.scalar.activation(junk[:, c, :], cen[:, p, c, :], ACT.Square, accum_out=var[:, p, c:c + 1])
                        ins.then_inc(square_done.sem, 1)
                        after(act, square_done, l, h)
                        nc.scalar.activation(lnv[:, :], var[:, p, :], ACT.Ln, bias=eps[:, 0:1], scale=1.0 / D).then_inc(lnv_done.sem, 1)
                        after(act, lnv_done, l, h)
                        nc.scalar.activation(rstd[:, p, :], lnv[:, :], ACT.Exp, scale=-0.5).then_inc(rstd_ready.sem, 1)

                    def exponentials(h):
                        p = h.par
                        after(act, dif_ready, l, h)
                        after(act, acc_step, l, h.plus(-2))
                        nc.scalar.activation(ex[:, p, :, 0:H * C], dif[:, p, :, 0:H * C], ACT.Exp, scale=SCALE).then_inc(exp_ready.sem, 1)

                    def aggregate(h):
                        after(act, agT_made, l, h)
                        after(act, wo_ready, l, h.plus(-1))
                        nc.scalar.copy(agT[:, :], psX[0][:, 0:2 * P]).then_inc(agT_ready.sem, 1)

                    def softmax_exp(h):
                        after(act, z_ready, l, h)
                        nc.scalar.activation(ez[:, :, :], t1[:, :, :], ACT.Exp).then_inc(ez_ready.sem, 1)

                    def logarithm(h):
                        after(act, esum_ready, l, h)
                        nc.scalar.activation(lns[:, :], esum[:, :], ACT.Ln).then_inc(ln_ready.sem, 1)

                    def step(h):
                        stage(queries, h, 0, HALVES)
                        if l == 2:
                            stage(softmax_exp, h, -2, HALVES)
                        if l == 3:
                            stage(aggregate, h, -2, HALVES)
                        stage(evacuate, h, 1, HALVES)
                        stage(indices, h, 3, HALVES)
                        stage(variance, h, -lag, HALVES)
                        if l == 2:
                            stage(logarithm, h, -2, HALVES)
                        stage(exponentials, h, 0, HALVES)
                        if l < 2:
                            stage(relu, h, -2, HALVES)
                        if l == 3:
                            stage(residual, h, 0, HALVES)
                    act.preload_act_table_set("natural_log_exp_and_others")
                    run(act, HALVES, step, -3, HALVES + lag - 1)
                    link, n = link_from(act, s_link, chain.get("act", 0))
                    act.wait_ge(w_ready.sem, at(w_ready, l))
                    link(nc.scalar.activation(ctile["e1"][0:RL, :], ctile["d1"][0:RL, :], ACT.Exp, scale=SCALE))
                    nc.scalar.activation(ctile["e2"][0:RL, :], ctile["d2"][0:RL, :], ACT.Exp, scale=SCALE).then_inc(w_exp.sem, 1)
                    act.wait_ge(m_ready.sem, at(m_ready, l))
                    link(nc.scalar.activation(ctile["e1"][0:RL, :], ctile["d1"][0:RL, :], ACT.Exp, scale=SCALE))
                    nc.scalar.activation(ctile["e2"][0:RL, :], ctile["d2"][0:RL, :], ACT.Exp, scale=SCALE).then_inc(m_exp.sem, 1)
                    if l == 2:
                        act.wait_ge(f_z.sem, at(f_z, l))
                        nc.scalar.activation(fc[:, :], fa[:, :], ACT.Exp).then_inc(f_ez.sem, 1)
                        act.wait_ge(f_es.sem, at(f_es, l))
                        nc.scalar.activation(fsm[:, 1:2], fsm[:, 0:1], ACT.Ln).then_inc(f_ln.sem, 1)
                    act.wait_ge(f_cen.sem, at(f_cen, l))
                    nc.scalar.activation(fc[:, :], fcen[:, :], ACT.Square, accum_out=fsm[:, 4:5]).then_inc(f_sq.sem, 1)
                    act.wait_ge(f_sq.sem, at(f_sq, l))
                    nc.scalar.activation(fsm[:, 5:6], fsm[:, 4:5], ACT.Ln, bias=eps[:, 0:1], scale=1.0 / D).then_inc(f_lv.sem, 1)
                    act.wait_ge(f_lv.sem, at(f_lv, l))
                    nc.scalar.activation(fsm[:, 6:7], fsm[:, 5:6], ACT.Exp, scale=-0.5).then_inc(f_rstd.sem, 1)
                    chain["act"] = n[0]

                @block.vector
                def _(dve):
                    tt, tsc = nc.vector.tensor_tensor, nc.vector.tensor_scalar

                    def kv_of(h):
                        return psKV[h.par][:, :].rearrange("p (c d) -> p c d", c=C)

                    def lead_part(h):
                        after(dve, xs_ready, l, h.plus(-1))
                        tt(leadx[:, :, :], wide(lead[:, h.cols()]), fix[:, :].unsqueeze(1).broadcast_to([P, C, D]), ALU.mult).then_inc(lead_x.sem, 1)

                    def inputs(h):
                        after(dve, transposed, l, h.plus(-2))
                        if l == 3:
                            after(dve, res_ready, l, h.plus(-2))
                        after(dve, lead_x, l, h)
                        tt(xs[:, h.par, :, :], leadx[:, :, :], feats[:, h.cols(), :], ALU.add).then_inc(xs_ready.sem, 1)

                    def qk_product(h):
                        after(dve, kv_ready, l, h)
                        after(dve, qs_ready, l, h)
                        tt(prod[:, :, :], kv_of(h)[:, :, 0:D], qs[:, h.par, :, 0:D], ALU.mult).then_inc(prod_done.sem, 1)

                    def scores(h):
                        after(dve, prod_done, l, h)
                        nc.vector.reduce_sum(heads(alpha[:, h.par, :]).rearrange("p h c -> p c h"), split(prod[:, :, :]), AX.X).then_inc(alpha_done.sem, 1)

                    def maxima(h):
                        j, am = h.k * C, heads(alpha[:, h.par, :])
                        after(dve, alpha_done, l, h)
                        if l == 3:
                            am = heads(alphac[:, :])
                            tsc(am, heads(alpha[:, h.par, :]), -1.0e9 / SCALE, None, ALU.max).then_inc(floor_done.sem, 1)
                            after(dve, floor_done, l, h)
                        for hd in range(H):
                            ins = nc.vector.tensor_tensor_scan(M[:, hd, bass.ds(j + 1, C)], pen[:, h.cols()], am[:, hd, :],
                                                               M[:, hd, bass.ds(j, 1)], ALU.add, ALU.max)
                        ins.then_inc(max_done.sem, 1)

                    def decays(h):
                        after(dve, max_done, l, h)
                        after(dve, dif_ready, l, h.plus(-1))
                        tt(heads(dif0[:, :]), M[:, 0:H, bass.ds(h.k * C, C)], pen[:, h.cols()].unsqueeze(1).broadcast_to([P, H, C]),
                           ALU.add).then_inc(dif0_done.sem, 1)

                    def exponents(h):
                        p, m = h.par, M[:, 0:H, bass.ds(h.k * C + 1, C)]
                        after(dve, exp_ready, l, h.plus(-2))
                        after(dve, dif0_done, l, h)
                        tt(heads(dif[:, p, 0, :]), heads(dif0[:, :]), m, ALU.subtract)
                        tt(heads(dif[:, p, 1, :]), heads(alpha[:, p, :]), m, ALU.subtract).then_inc(dif_ready.sem, 1)

                    def totals(h):
                        p, j = h.par, h.k * C
                        decay, weight = heads(ex[:, p, 0, :]), heads(ex[:, p, 1, :])
                        after(dve, exp_ready, l, h)
                        for hd in range(H):
                            ins = nc.vector.tensor_tensor_scan(S[:, hd, bass.ds(j + 1, C)], decay[:, hd, :], weight[:, hd, :],
                                                               S[:, hd, bass.ds(j, 1)], ALU.mult, ALU.add)
                        ins.then_inc(sum_done.sem, 1)

                    def weighted(h):
                        after(dve, exp_ready, l, h)
                        after(dve, acc_step, l, h.plus(-1))
                        tt(split(pv[:, :, :]), split(kv_of(h)[:, :, D:2 * D]), over_features(heads(ex[:, h.par, 1, :])), ALU.mult).then_inc(pv_done.sem, 1)

                    def accumulate(c):
                        def piece(h):
                            p, decay = h.par, heads(ex[:, h.par, 0, :])
                            before = acc[:, (p * C + c - 1) % (2 * C), :]
                            if c == 0:
                                after(dve, pv_done, l, h)
                                landed(dve, acc_out, l, h.plus(-2))
                            wait(dve, acc_step.sem, acc_step.at(l, h.k, c))
                            if l < 3:
                                ins = nc.vector.scalar_tensor_tensor(acc[:, p * C + c, :], before, decay[:, 0, c:c + 1], pv[:, c, :],
                                                                     ALU.mult, ALU.add)
                            else:
                                tt(carry[:, :].rearrange("p (h f) -> p h f", h=H), before.rearrange("p (h f) -> p h f", h=H),
                                   decay[:, :, c:c + 1].broadcast_to([P, H, F]), ALU.mult).then_inc(carried.sem, 1)
                                wait(dve, carried.sem, carried.at(l, h.k, c + 1))
                                ins = tt(acc[:, p * C + c, :], carry[:, :], pv[:, c, :], ALU.add)
                            ins.then_inc(acc_step.sem, 1)
                        return piece

                    acc0, acc1, acc2, acc3 = (accumulate(c) for c in range(C))

                    def divisors(h):
                        after(dve, sum_done, l, h)
                        after(dve, sinv_done, l, h.plus(-1))
                        tsc(heads(stot[:, :]), S[:, 0:H, bass.ds(h.k * C + 1, C)], 1.0e-9 if l == 3 else 0.0, None, ALU.add).then_inc(seps_done.sem, 1)

                    def inverses(h):
                        after(dve, norm_done, l, h.plus(-1))
                        after(dve, seps_done, l, h)
                        nc.vector.reciprocal(heads(sinv[:, :]), heads(stot[:, :])).then_inc(sinv_done.sem, 1)

                    def aggregates(h):
                        p = h.par
                        after(dve, sinv_done, l, h)
                        after(dve, acc_step, l, h)
                        if l == 2:
                            after(dve, lsm_done, l, h.plus(-1))
                        if l == 3:
                            after(dve, agT_made, l, h.plus(-1))
                        tt(split(t1[:, :, :]), split(acc[:, p * C:(p + 1) * C, :]), over_features(heads(sinv[:, :])), ALU.mult).then_inc(norm_done.sem, 1)

                    def skip_added(h):
                        if l < 3:
                            after(dve, norm_done, l, h)
                            after(dve, relu_done, l, h.plus(-1))
                            tt(t2[:, :, :], t1[:, :, :], qs[:, h.par, :, D:2 * D], ALU.add).then_inc(added.sem, 1)
                        else:
                            after(dve, wo_ready, l, h)
                            after(dve, res_ready, l, h)
                            tt(t3[:, :, :], psX[1][:, 0:C * D].rearrange("p (c d) -> p c d", c=C), x0[:, h.par, :, :], ALU.add).then_inc(added.sem, 1)

                    def relu(h):
                        after(dve, z_ready, l, h.plus(-1))
                        after(dve, added, l, h)
                        tsc(yout[:, 0], t2[:, :, :], 0.0, None, ALU.max).then_inc(relu_done.sem, 1)

                    def row_maxima(h):
                        after(dve, relu_done, l, h)
                        nc.vector.reduce_max(hmax[:, :], yout[:, 0], AX.X).then_inc(hmax_done.sem, 1)

                    def less_maximum(h):
                        after(dve, hmax_done, l, h)
                        tt(t1[:, :, :], yout[:, 0], wide(hmax[:, :]), ALU.subtract).then_inc(z_ready.sem, 1)

                    def exp_sum(h):
                        after(dve, ez_ready, l, h)
                        nc.vector.reduce_sum(esum[:, :], ez[:, :, :], AX.X).then_inc(esum_ready.sem, 1)

                    def less_log(h):
                        after(dve, ln_ready, l, h)
                        after(dve, res_done, l, h.plus(-1))
                        tt(yout[:, 1], t1[:, :, :], wide(lns[:, :]), ALU.subtract).then_inc(lsm_done.sem, 1)

                    def x0_added(h):
                        after(dve, cen_ready, l, h.plus(-1))
                        after(dve, lsm_done, l, h)
                        landed(dve, x0_in, l, h)
                        tt(t3[:, :, :], yout[:, 1], x0[:, h.par, :, :], ALU.add).then_inc(res_done.sem, 1)

                    def row_sums(h):
                        after(dve, res_done if l == 2 else added, l, h)
                        nc.vector.reduce_sum(csum[:, h.par, :], t3[:, :, :], AX.X).then_inc(fsum_done.sem, 1)

                    def means(h):
                        after(dve, fsum_done if l > 1 else relu_done, l, h)
                        tsc(mean[:, :], csum[:, h.par, :], 1.0 / D, None, ALU.mult).then_inc(mean_done.sem, 1)

                    def centred(h):
                        after(dve, mean_done, l, h)
                        after(dve, value_ready, l, h.plus(-2))
                        tt(cen[:, h.par, :, :], t3[:, :, :] if l > 1 else yout[:, h.par], wide(mean[:, :]), ALU.subtract).then_inc(cen_ready.sem, 1)

                    def row_scales(h):
                        after(dve, rstd_ready, l, h)
                        after(dve, value_ready, l, h.plus(-1))
                        tt(rmask[:, :], rstd[:, h.par, :], ownlast[:, h.cols()], ALU.mult).then_inc(rmask_done.sem, 1)

                    def values(h):
                        p = h.par
                        after(dve, rmask_done, l, h)
                        if l == 3:
                            landed(dve, out_done, l, h.plus(-2))
                            nc.vector.tensor_copy(oidx[:, p, :], out_i[:, h.cols()]).then_inc(oidx_ready.sem, 1)
                        target = feats[:, h.cols(), :] if l < 3 else yout[:, p, :, :]
                        tt(target, cen[:, p, :, :], wide(rmask[:, :]), ALU.mult).then_inc(value_ready.sem, 1)

                    pieces = [(weighted, -1), (qk_product, 0), (totals, -1), (acc0, -1), (scores, 0), (acc1, -1)]
                    if l == 2:
                        pieces += [(exp_sum, -2)]
                    pieces += [(lead_part, 2)] * (l == 1) + [(maxima, 0), (acc2, -1), (decays, 0), (acc3, -1), (exponents, 0), (divisors, -1)]
                    pieces += [(row_scales, -lag), (inverses, -1)]
                    pieces += [(less_log, -2)] * (l == 2) + [(values, -lag)]
                    if l < 2:
                        pieces += [(aggregates, -1), (means, -2), (centred, -2), (skip_added, -1)]
                    elif l == 2:
                        pieces += [(aggregates, -1), (x0_added, -2), (skip_added, -1), (row_sums, -2), (relu, -1), (means, -2),
                                   (row_maxima, -1), (centred, -2), (less_maximum, -1)]
                    else:
                        pieces += [(skip_added, -2), (aggregates, -1), (row_sums, -2), (lead_part, 2), (means, -2), (inputs, 2), (centred, -2)]

                    def step(h):
                        for piece, off in pieces:
                            stage(piece, h, off, HALVES)
                    run(dve, HALVES, step, -2, HALVES + lag - 1)

                    link, n = link_from(dve, c_link, chain.get("dve", 0))
                    after(dve, value_ready, l, Half(HALVES // 2 - 1, 1))
                    after(dve, max_done, l, Half(HALVES // 2 - 1, 1))
                    lm = leadend[:, :].unsqueeze(1).broadcast_to([P, H, COLS])
                    link(tt(big[:, 0:H, :], M[:, 0:H, 1:COLS + 1], lm, ALU.mult))
                    link(nc.vector.reduce_sum(fsm[:, 0:H], big[:, 0:H, :], AX.X))
                    hb = [P, H, F]

                    def spread(tile, small):
                        link(nc.vector.tensor_copy(tile[:, 0:D].rearrange("p (h f) -> p h f", h=H), small.unsqueeze(2).broadcast_to(hb)))
                        link(nc.vector.tensor_copy(tile[:, D:RL], small))
                    spread(rmF, fsm[:, 0:H])
                    link(nc.vector.tensor_copy(fsm[:, 4:4 + H], M[:, 0:H, COLS:COLS + 1].rearrange("p h o -> p (h o)")))
                    spread(rm, fsm[:, 4:4 + H])
                    link(tt(big[:, 0:H, :], S[:, 0:H, 1:COLS + 1], lm, ALU.mult))
                    link(nc.vector.memset(rf[:, :], 0.0))
                    link(nc.vector.memset(rx[:, :, :], 0.0))
                    nc.vector.reduce_sum(rf[:, D:RL], big[:, 0:H, :], AX.X).then_inc(fix_preset.sem, 1)
                    dve.wait_ge(fix_preset.sem, at(fix_preset, l))
                    link(nc.vector.tensor_copy(ra[:, 0:D], acc[:, 2 * C - 1, :]))
                    link(nc.vector.tensor_copy(ra[:, D:RL], S[:, 0:H, COLS:COLS + 1].rearrange("p h o -> p (h o)")))
                    dve.wait_ge(fix_in, 48 * (l + 1) if l < 3 else 48 * 3 + 16)
                    nc.vector.tensor_copy(fsm[:, 0:1], ends[:, 0:1]).then_inc(ends_ready.sem, 1)
                    dve.wait_ge(ends_T.sem, at(ends_T, l))
                    c = {k: v[0:RL, :] for k, v in ctile.items()}
                    for j, k in enumerate(("m", "a", "mF", "f")):
                        link(nc.vector.tensor_copy(c[k], psT[0][0:RL, j * P:(j + 1) * P]))
                    link(nc.vector.memset(cG[:, 0:1], NEVER))
                    link(nc.vector.memset(cA[:, 0:1], 0.0))
                    g0, g1 = cG[0:RL, 0:P], cG[0:RL, 1:P + 1]
                    link(nc.vector.tensor_tensor_scan(g1, c["wpen"], c["m"], NEVER, ALU.add, ALU.max))
                    link(tt(c["t"], g0, c["wpen"], ALU.add))
                    link(tt(c["d1"], c["t"], g1, ALU.subtract))
                    tt(c["d2"], c["m"], g1, ALU.subtract).then_inc(w_ready.sem, 1)
                    dve.wait_ge(w_exp.sem, at(w_exp, l))
                    link(tt(c["t"], c["e2"], c["a"], ALU.mult))
                    link(nc.vector.tensor_tensor_scan(cA[0:RL, 1:P + 1], c["e1"], c["t"], 0.0, ALU.mult, ALU.add))
                    link(tt(c["a"], g0, c["cpen"], ALU.add))
                    link(tt(c["t"], c["a"], c["mF"], ALU.max))
                    link(tt(c["d1"], c["a"], c["t"], ALU.subtract))
                    tt(c["d2"], c["mF"], c["t"], ALU.subtract).then_inc(m_ready.sem, 1)
                    dve.wait_ge(m_exp.sem, at(m_exp, l))
                    link(tt(c["a"], cA[0:RL, 0:P], c["e1"], ALU.mult))
                    link(tt(c["m"], c["f"], c["e2"], ALU.mult))
                    tt(c["t"], c["a"], c["m"], ALU.add).then_inc(tot_ready.sem, 1)
                    dve.wait_ge(tot_T.sem, at(tot_T, l))
                    link(tsc(fsm[:, 0:H], psT[1][:, D:RL], ends[:, 1:2], 1.0e-9 if l == 3 else None, ALU.add,
                             *([ALU.add] if l == 3 else [])))
                    link(nc.vector.reciprocal(fsm[:, 4:4 + H], fsm[:, 0:H]))
                    link(tt(fb[:, :].rearrange("p (h f) -> p h f", h=H), psT[1][:, 0:D].rearrange("p (h f) -> p h f", h=H),
                            fsm[:, 4:4 + H].unsqueeze(2).broadcast_to(hb), ALU.mult))
                    if l < 3:
                        link(tt(fc[:, :], fb[:, :], rx[:, 0, :], ALU.add))
                        link(tsc(fb[:, :], fc[:, :], 0.0, None, ALU.max))
                    else:
                        nc.vector.tensor_copy(fa[:, :], fb[:, :]).then_inc(f_agg.sem, 1)
                        dve.wait_ge(f_aggT.sem, at(f_aggT, l))
                        nc.vector.tensor_copy(faggT[0:D, :], psX[0][0:D, 0:P]).then_inc(f_aggTs.sem, 1)
                        dve.wait_ge(f_wo.sem, at(f_wo, l))
                        link(tt(fb[:, :], psX[1][:, 0:D], fix[:, :], ALU.add))
                    if l == 2:
                        link(nc.vector.reduce_max(fsm[:, 0:1], fb[:, :], AX.X))
                        tsc(fa[:, :], fb[:, :], fsm[:, 0:1], None, ALU.subtract).then_inc(f_z.sem, 1)
                        dve.wait_ge(f_ez.sem, at(f_ez, l))
                        nc.vector.reduce_sum(fsm[:, 0:1], fc[:, :], AX.X).then_inc(f_es.sem, 1)
                        dve.wait_ge(f_ln.sem, at(f_ln, l))
                        link(tsc(fc[:, :], fa[:, :], fsm[:, 1:2], None, ALU.subtract))
                        link(tt(fb[:, :], fc[:, :], rx[:, 1, :], ALU.add))
                    link(nc.vector.reduce_sum(fsm[:, 2:3], fb[:, :], AX.X))
                    link(tsc(fsm[:, 3:4], fsm[:, 2:3], 1.0 / D, None, ALU.mult))
                    tsc(fcen[:, :], fb[:, :], fsm[:, 3:4], None, ALU.subtract).then_inc(f_cen.sem, 1)
                    dve.wait_ge(f_rstd.sem, at(f_rstd, l))
                    tsc(fix[:, :], fcen[:, :], fsm[:, 6:7], ends[:, 0:1], ALU.mult, ALU.mult).then_inc(fix_ready.sem, 1)
                    if l < 3:
                        dve.wait_ge(fix_T.sem, at(fix_T, l))
                        link(nc.vector.memset(cR[:, P:P + 1], 0.0))
                        link(nc.vector.tensor_copy(ctile["a"][0:D, :], psX[0][0:D, 0:P]))
                        nc.vector.tensor_tensor_scan(cR[:, 0:P][:, ::-1], ctile["noend"][0:D, ::-1], ctile["a"][0:D, ::-1], 0.0,
                                                     ALU.mult, ALU.add).then_inc(init_ready.sem, 1)
                        dve.wait_ge(init_T.sem, at(init_T, l))
                        link(nc.vector.tensor_copy(init[:, :], psX[1][:, 0:D]))
                        for p in (0, 1):
                            landed(dve, rows_out, l, Half(HALVES // 2 - 1, p))
                        for f in range(D):
                            ins = nc.vector.tensor_tensor_scan(feats[:, ::-1, f], notlast[:, ::-1], feats[:, ::-1, f], init[:, f:f + 1],
                                                               ALU.mult, ALU.add)
                        link(ins)
                    chain["dve"] = n[0]


_INS = ["x", "src", "dst", "edge_attr_64", "L0_gnn_Wq", "L0_gnn_bq", "L0_gnn_Wk", "L0_gnn_bk", "L0_gnn_Wv", "L0_gnn_bv",
        "L0_gnn_We", "L0_gnn_Ws", "L0_gnn_bs", "L0_gnn_ln_gamma", "L0_gnn_ln_beta", "L1_gnn_Wq", "L1_gnn_Wk", "L1_gnn_Wv",
        "L1_gnn_Wo"]


def kernel(**inputs):
    import numpy as np
    import concourse.bacc as bacc
    from concourse.bass_utils import run_bass_kernel_spmd

    nc = bacc.Bacc("TRN2", target_bir_lowering=False, num_devices=1)
    arrays, args = {}, []
    for name in _INS:
        a = np.ascontiguousarray(inputs[name])
        arrays[f"in_{name}"] = a
        args.append(nc.dram_tensor(f"in_{name}", a.shape, mybir.dt.from_np(a.dtype), kind="ExternalInput").ap())
    out = nc.dram_tensor("out_0", inputs["x"].shape, F32, kind="ExternalOutput").ap()
    gnn_kernel(nc, *args, out)
    return run_bass_kernel_spmd(nc, [arrays], core_ids=[0]).results[0]["out_0"]
```
